# Optimizing a Trainium2 kernel written in Bass

```python
import numpy as np
import jax
import jax.numpy as jnp

def _softmax(x, axis=-1):
    return jax.nn.softmax(x, axis=axis)

def _gelu(x):
    return jax.nn.gelu(x, approximate=True)

def _silu(x):
    return jax.nn.silu(x)

def _sigmoid(x):
    return jax.nn.sigmoid(x)

def _layernorm(x, axis=-1, eps=1e-05):
    m = jnp.mean(x, axis=axis, keepdims=True)
    v = jnp.var(x, axis=axis, keepdims=True)
    return (x - m) / jnp.sqrt(v + eps)

def _scatter_add(tgt, idx, src, axis=0):
    return tgt.at[idx].add(src)

def _segment_sum(src, seg, n):
    return jax.ops.segment_sum(src, seg, n)
kernel_name = 'mk_conv_attn_hybrid_d2_conv_nhwc128_r4_824e5c'

def setup_inputs(seed: int=0):
    np.random.seed(seed)
    _w = jnp.asarray

    def _rec_inputs():
        import jax
        import jax.numpy as jnp
        _gk = jax.random.key(seed)
        x = 7.22e-05 + 1 * jax.random.normal(jax.random.fold_in(_gk, 1), (16, 16, 16, 32), jnp.float32)
        return x
    x = _rec_inputs()

    def _L0_conv_setup():
        import jax, jax.numpy as jnp
        import numpy as np
        HEADS = 4
        DIM_HEAD = 32
        EPS = 1e-05
        key = jax.random.key(seed)
        ks = jax.random.split(key, 3)
        B, H, W, C = (16, 16, 16, 32)
        hidden = HEADS * DIM_HEAD
        x = jax.random.normal(ks[0], (B, H, W, C), dtype=jnp.float32)
        w_qkv = jax.random.normal(ks[1], (C, 3 * hidden), dtype=jnp.float32) * 0.05
        w_out = jax.random.normal(ks[2], (hidden, C), dtype=jnp.float32) * 0.05
        b_out = jnp.zeros((C,), dtype=jnp.float32)
        g_ln = jnp.ones((C,), dtype=jnp.float32)
        b_ln = jnp.zeros((C,), dtype=jnp.float32)
        return {'x': x, 'w_qkv': w_qkv, 'w_out': w_out, 'b_out': b_out, 'g_ln': g_ln, 'b_ln': b_ln}
    _L0_conv_all = _L0_conv_setup()
    _L0_conv_in = {k: v for k, v in _L0_conv_all.items() if k in ('w_qkv', 'w_out', 'b_out', 'g_ln', 'b_ln')}
    del _L0_conv_all

    def _L1_attn_setup():
        import jax, jax.numpy as jnp
        import numpy as np
        B, T, C = (16, 512, 32)
        HEAD_SIZE = 32
        key = jax.random.key(seed)
        k1, k2, k3, k4 = jax.random.split(key, 4)
        x = jax.random.normal(k1, (B, T, C), dtype=jnp.float32)
        scale = (1.0 / np.sqrt(C)).astype(np.float32)
        Wq = jax.random.normal(k2, (HEAD_SIZE, C), dtype=jnp.float32) * scale
        Wk = jax.random.normal(k3, (HEAD_SIZE, C), dtype=jnp.float32) * scale
        Wv = jax.random.normal(k4, (HEAD_SIZE, C), dtype=jnp.float32) * scale
        return {'x': x, 'Wq': Wq, 'Wk': Wk, 'Wv': Wv}
    _L1_attn_all = _L1_attn_setup()
    _L1_attn_in = {k: v for k, v in _L1_attn_all.items() if k in ('Wq', 'Wk', 'Wv')}
    del _L1_attn_all

    def _L1_ffn_setup():
        import jax, jax.numpy as jnp
        import numpy as np
        BN_EPS = 1e-05
        key = jax.random.key(seed)
        k1, k2, k3 = jax.random.split(key, 3)
        B, T, I, H = (16, 512, 32, 32)
        x = jax.random.normal(k1, (B, T, I), dtype=jnp.float32)
        W = jax.random.normal(k2, (H, I), dtype=jnp.float32) * (1.0 / np.sqrt(I))
        V = jnp.linalg.qr(jax.random.normal(k3, (H, H), dtype=jnp.float32))[0]
        gamma = jnp.ones((H,), dtype=jnp.float32)
        beta = jnp.zeros((H,), dtype=jnp.float32)
        return {'x': x, 'W': W, 'V': V, 'gamma': gamma, 'beta': beta}
    _L1_ffn_all = _L1_ffn_setup()
    _L1_ffn_in = {k: v for k, v in _L1_ffn_all.items() if k in ('W', 'V', 'gamma', 'beta')}
    del _L1_ffn_all
    return {'x': x, 'L0_conv_w_qkv': _L0_conv_in['w_qkv'], 'L0_conv_w_out': _L0_conv_in['w_out'], 'L0_conv_b_out': _L0_conv_in['b_out'], 'L0_conv_g_ln': _L0_conv_in['g_ln'], 'L0_conv_b_ln': _L0_conv_in['b_ln'], 'L1_attn_Wq': _L1_attn_in['Wq'], 'L1_attn_Wk': _L1_attn_in['Wk'], 'L1_attn_Wv': _L1_attn_in['Wv'], 'L1_ffn_W': _L1_ffn_in['W'], 'L1_ffn_V': _L1_ffn_in['V'], 'L1_ffn_gamma': _L1_ffn_in['gamma'], 'L1_ffn_beta': _L1_ffn_in['beta']}

def reference(x, L0_conv_w_qkv, L0_conv_w_out, L0_conv_b_out, L0_conv_g_ln, L0_conv_b_ln, L1_attn_Wq, L1_attn_Wk, L1_attn_Wv, L1_ffn_W, L1_ffn_V, L1_ffn_gamma, L1_ffn_beta):
    import jax
    import jax.numpy as jnp

    def _L0_conv_ref(x, w_qkv, w_out, b_out, g_ln, b_ln):
        import jax, jax.numpy as jnp
        import numpy as np
        HEADS = 4
        DIM_HEAD = 32
        EPS = 1e-05
        B, H, W, C = x.shape
        scale = DIM_HEAD ** (-0.5)
        n = H * W
        qkv = jnp.einsum('bhwc,cf->bhwf', x, w_qkv)
        q, k, v = jnp.split(qkv, 3, axis=-1)

        def to_heads(t):
            return t.reshape(B, n, HEADS, DIM_HEAD).transpose(0, 2, 3, 1)
        q, k, v = map(to_heads, (q, k, v))
        q = jax.nn.softmax(q, axis=-2) * scale
        k = jax.nn.softmax(k, axis=-1)
        context = jnp.einsum('bhdn,bhen->bhde', k, v)
        out = jnp.einsum('bhde,bhdn->bhen', context, q)
        out = out.transpose(0, 3, 1, 2).reshape(B, H, W, HEADS * DIM_HEAD)
        out = jnp.einsum('bhwc,cd->bhwd', out, w_out) + b_out
        mean = jnp.mean(out, axis=-1, keepdims=True)
        var = jnp.var(out, axis=-1, keepdims=True)
        out = (out - mean) / jnp.sqrt(var + EPS) * g_ln + b_ln
        return out

    def _L1_attn_ref(x, Wq, Wk, Wv):
        import jax, jax.numpy as jnp
        import numpy as np
        B, T, C = (16, 512, 32)
        HEAD_SIZE = 32
        Bd, Td, Cd = x.shape
        q = jnp.einsum('btc,hc->bth', x, Wq)
        k = jnp.einsum('btc,hc->bth', x, Wk)
        v = jnp.einsum('btc,hc->bth', x, Wv)
        scores = jnp.einsum('bth,bsh->bts', q, k) * Cd ** (-0.5)
        causal = jnp.tril(jnp.ones((Td, Td), dtype=bool))
        scores = jnp.where(causal, scores, -jnp.inf)
        attn = jax.nn.softmax(scores, axis=-1)
        out = jnp.einsum('bts,bsh->bth', attn, v)
        return out

    def _L1_ffn_ref(x, W, V, gamma, beta):
        import jax, jax.numpy as jnp
        import numpy as np
        BN_EPS = 1e-05
        B, T, H = (x.shape[0], x.shape[1], W.shape[0])
        Wx = jnp.einsum('bti,hi->bth', x, W)
        flat = Wx.reshape(B * T, H)
        mean = jnp.mean(flat, axis=0)
        var = jnp.var(flat, axis=0)
        Wx = ((flat - mean) * jax.lax.rsqrt(var + BN_EPS) * gamma + beta).reshape(B, T, H)
        Vt = V.T

        def step(yt, wx_t):
            yt = jax.nn.sigmoid(wx_t + yt @ Vt)
            return (yt, yt)
        y0 = jnp.zeros((B, H), dtype=Wx.dtype)
        _, ys = jax.lax.scan(step, y0, jnp.swapaxes(Wx, 0, 1))
        return jnp.swapaxes(ys, 0, 1)

    def _gn(v, G=32, eps=1e-05):
        B_, H_, W_, C_ = v.shape
        g = v.reshape(B_, H_, W_, G, C_ // G)
        m = jnp.mean(g, axis=(1, 2, 4), keepdims=True)
        s = jnp.var(g, axis=(1, 2, 4), keepdims=True)
        return ((g - m) / jnp.sqrt(s + eps)).reshape(v.shape)

    def _ln_c(v, eps=1e-06):
        m = jnp.mean(v, axis=-1, keepdims=True)
        s = jnp.var(v, axis=-1, keepdims=True)
        return (v - m) / jnp.sqrt(s + eps)

    def _ln_t(v, eps=1e-05):
        m = jnp.mean(v, axis=-1, keepdims=True)
        s = jnp.var(v, axis=-1, keepdims=True)
        return (v - m) / jnp.sqrt(s + eps)

    def _to_tokens(v):
        B_, H_, W_, C_ = v.shape
        return v.reshape(B_, H_ * W_, C_)

    def _from_tokens(t, like):
        return t.reshape(like.shape)
    x = x + _L0_conv_ref(_gn(x), L0_conv_w_qkv, L0_conv_w_out, L0_conv_b_out, L0_conv_g_ln, L0_conv_b_ln)
    t = _to_tokens(x)
    t = t + _L1_attn_ref(_ln_t(t), L1_attn_Wq, L1_attn_Wk, L1_attn_Wv)
    t = t + _L1_ffn_ref(_ln_t(t), L1_ffn_W, L1_ffn_V, L1_ffn_gamma, L1_ffn_beta)
    x = _from_tokens(t, x)
    return x

_drawn_inputs = setup_inputs


def setup_inputs(seed=0):
    import zlib

    import numpy as np

    out = dict(_drawn_inputs(seed))
    spreads = {'L0_conv_b_out': (0.0, 0.1),
     'L0_conv_g_ln': (1.0, 0.2),
     'L0_conv_b_ln': (0.0, 0.1),
     'L1_ffn_gamma': (1.0, 0.6),
     'L1_ffn_beta': (0.0, 0.782)}
    factors = {'L0_conv_w_qkv': 8.0, 'L0_conv_w_out': 8.0}
    for name, (base, spread) in spreads.items():
        noise = np.random.default_rng([zlib.crc32(name.encode()), seed]).standard_normal(out[name].shape)
        drawn = base * np.exp(spread * noise) if base else spread * noise
        out[name] = jnp.asarray(drawn.astype(out[name].dtype))
    for name, factor in factors.items():
        out[name] = (out[name] * factor).astype(out[name].dtype)
    return out
```

```python
from contextlib import ExitStack

import numpy as np

import concourse.bass as bass
from concourse import mybir

ALU = mybir.AluOpType
ACT = mybir.ActivationFunctionType
F32 = mybir.dt.float32
BF16 = mybir.dt.bfloat16
I32 = mybir.dt.int32
AX_X = mybir.AxisListType.X

P = 128


def conv_attn_rnn(nc, x, w_qkv, w_out, b_out, g_ln, b_ln, w_q, w_k, w_v, w_ffn, v_ffn, gamma, beta, out):
    B, HH, WW, C = x.shape
    T = HH * WW
    G = P // C
    R = B // G
    HALVES = T // P
    HEADS = w_out.shape[0] // C
    TW = HALVES * P
    RC = G * HALVES * C
    ATTN_SCALE = float(C) ** -0.5
    MASKED = -1e30
    EPS = 1e-5
    assert (P, G, R, HALVES, HEADS) == (128, 4, 4, 2, 4)

    STRIDE = 4
    CHUNKS = T // STRIDE
    WARM = 12
    LEAD = WARM // STRIDE
    STEPS = WARM + STRIDE
    CHAINS = 2
    RPC = R // CHAINS
    AGREE = 2.0 ** -20

    with ExitStack() as ctx:
        def sb(name, shape, dt=F32):
            return ctx.enter_context(nc.sbuf_tensor(name, shape, dt))

        def sem(name):
            return ctx.enter_context(nc.semaphore(name))

        bank = [ctx.enter_context(nc.psum_tensor(f"bank{i}", [P, 512], F32)) for i in range(8)]

        x_tok = sb("x_tok", [P, R, HALVES, G, C])
        wqkv4 = sb("wqkv4", [P, 3 * P])
        wqk4_b = sb("wqk4_b", [P, 2 * P], BF16)
        wout_sb = sb("wout_sb", [P, C])
        wout_sum = sb("wout_sum", [P, 1])
        wout_c = sb("wout_c", [P, C])
        wout_bd = sb("wout_bd", [P, HEADS, C])
        wv_t = sb("wv_t", [P, C])
        proj = sb("proj", [C + 1, P + 1])
        brow = sb("brow", [C + 1, C])
        bsum = sb("bsum", [C + 1, 1])
        gln_bc = sb("gln_bc", [P, C])
        bln_bc = sb("bln_bc", [P, C])
        gam4 = sb("gam4", [P, 1])
        bet4 = sb("bet4", [P, 1])
        small4 = sb("small4", [P, 5, C])
        small_bd = sb("small_bd", [P, 5, G, C])
        wvT_bd = sb("wvT_bd", [P, P])
        wT_bd = sb("wT_bd", [P, P])
        vT_bd = sb("vT_bd", [P, P])
        score_bd = sb("score_bd", [P, P])

        ident = sb("ident", [P, P])
        ident_b = sb("ident_b", [P, P], BF16)
        negid_b = sb("negid_b", [P, P], BF16)
        blockmask = sb("blockmask", [P, HEADS, C])
        groupavg = sb("groupavg", [P, G, C])
        ones_f = sb("ones_f", [P, 1])
        halfneg = sb("halfneg", [P, 8])
        sel32 = sb("sel32", [P, 8, P], BF16)
        sel4 = sb("sel4", [P, G, P], BF16)
        sel8 = sb("sel8", [P, 8, P], BF16)
        mask_ts = sb("mask_ts", [P, P], BF16)
        mask_st = sb("mask_st", [P, P], BF16)

        gn_stats = sb("gn_stats", [P, R, 6])
        gn_mv = sb("gn_mv", [P, R, 2])
        gn_ve = sb("gn_ve", [P, R])
        gn_rs = sb("gn_rs", [P, R])
        xnT = sb("xnT", [P, R, TW])
        xnT_b = sb("xnT_b", [P, R, TW], BF16)
        xn1 = sb("xn1", [P, R, HALVES, G, C + 1])
        xb = sb("xb", [P, R, G * HALVES, C])

        qmax_b = sb("qmax_b", [P, R, HALVES, G, HEADS], BF16)
        kmax_b = sb("kmax_b", [P, R, G], BF16)
        qshift = sb("qshift", [P, R, P], BF16)
        kshift = sb("kshift", [P, R, P], BF16)
        eqk = sb("eqk", [P, R, G, 512])
        gram = sb("gram", [C + 1, R, G * P])
        ksum_r = sb("ksum_r", [P, R, G])
        ctxo = sb("ctxo", [P, R, G, P + HEADS])
        qsum_r = sb("qsum_r", [P, R, G, HALVES * HEADS])
        z4 = sb("z4", [P, R, G * HALVES, HEADS * C])
        z = sb("z", [P, R, G * HALVES, C])
        zg = sb("zg", [P, R, G * HALVES, C])

        sq = sb("sq", [P, 3, R, G * HALVES, C])
        ln_sum = sb("ln_sum", [P, 3, R, G * HALVES])
        ln_mean = sb("ln_mean", [P, 3, R, G * HALVES])
        ln_ve = sb("ln_ve", [P, 3, R, G * HALVES])
        ln_rs = sb("ln_rs", [P, 3, R, G * HALVES])
        t1 = sb("t1", [P, R, G * HALVES, C])
        tc = sb("tc", [P, 2, R, G * HALVES, C])
        tn = sb("tn", [P, 2, R, HALVES, G, C])

        tnT = sb("tnT", [P, R, TW])
        tnT_b = sb("tnT_b", [P, R, TW], BF16)
        uT = sb("uT", [P, R, TW])
        uT_b = sb("uT_b", [P, R, TW], BF16)
        v1 = sb("v1", [P, R, HALVES, G, C + 1])
        smax_b = sb("smax_b", [P, R, HALVES, G], BF16)
        sshift = sb("sshift", [P, R, P], BF16)
        probsT = eqk[:, :, :, 0:3 * P]
        psum_r = sb("psum_r", [P, R, G * HALVES])
        attn = sb("attn", [P, R, G * HALVES, C])
        t2 = sb("t2", [P, R, G * HALVES, C])
        tn2T = sb("tn2T", [P, R, TW])
        wxT = sb("wxT", [P, R, TW])

        bn_stats = sb("bn_stats", [P, R, 6])
        bn_mv = sb("bn_mv", [P, 2])
        bn_in = sb("bn_in", [P, 2])
        bn_tot = sb("bn_tot", [P, 2])
        bn_sc = sb("bn_sc", [P, 8])
        wxn = sb("wxn", [P, STRIDE, R, CHUNKS])
        ys = sb("ys", [P, R, CHUNKS, STRIDE])
        warm = sb("warm", [P, WARM, R, CHUNKS])
        out_tok = sb("out_tok", [P, R, HALVES, G, C])
        diff = sb("diff", [P, R, CHUNKS - 1])
        worst = sb("worst", [P, 2])
        again = sb("again", [1, 1], I32)
        state = sb("state", [P, R, STRIDE])

        s_x = [sem(f"s_x{r}") for r in range(R)]
        s_wqkv = sem("s_wqkv")
        s_wout = sem("s_wout")
        s_small = sem("s_small")
        s_lnp = sem("s_lnp")
        s_ident = sem("s_ident")
        s_const = sem("s_const")
        s_pool = sem("s_pool")
        s_dve = sem("s_dve")
        s_xT = sem("s_xT")
        s_gnve = sem("s_gnve")
        s_gnrs = sem("s_gnrs")
        s_xnT = sem("s_xnT")
        s_xnTb = sem("s_xnTb")
        s_xnk = sem("s_xnk")
        s_xn1 = sem("s_xn1")
        s_xb = sem("s_xb")
        s_wqkb = sem("s_wqkb")
        s_wprep = sem("s_wprep")
        s_wpe = sem("s_wpe")
        s_wev = sem("s_wev")
        s_maxA = sem("s_maxA")
        s_redA = sem("s_redA")
        s_negA = sem("s_negA")
        s_shA = sem("s_shA")
        s_qk = sem("s_qk")
        s_expA = sem("s_expA")
        s_gram = sem("s_gram")
        s_gramS = sem("s_gramS")
        s_ctx = sem("s_ctx")
        s_ctxS = sem("s_ctxS")
        s_out = sem("s_out")
        s_z4 = sem("s_z4")
        s_z = sem("s_z")
        s_zg = sem("s_zg")
        s_sqin = [sem(f"s_sqin{n}") for n in range(3)]
        s_sq = [sem(f"s_sq{n}") for n in range(3)]
        s_ve = [sem(f"s_ve{n}") for n in range(3)]
        s_rs = [sem(f"s_rs{n}") for n in range(3)]
        s_tn = [sem(f"s_tn{n}") for n in range(2)]
        s_T = sem("s_T")
        s_tnT = sem("s_tnT")
        s_tnTb = sem("s_tnTb")
        s_u = sem("s_u")
        s_uT = sem("s_uT")
        s_uTb = sem("s_uTb")
        s_v = sem("s_v")
        s_v1 = sem("s_v1")
        s_maxB = sem("s_maxB")
        s_redB = sem("s_redB")
        s_negB = sem("s_negB")
        s_shB = sem("s_shB")
        s_st = sem("s_st")
        s_expB = sem("s_expB")
        s_pv = sem("s_pv")
        s_attn = sem("s_attn")
        s_T2 = sem("s_T2")
        s_tn2T = sem("s_tn2T")
        s_wx = sem("s_wx")
        s_wxS = sem("s_wxS")
        s_bnin = sem("s_bnin")
        s_bnp = sem("s_bnp")
        s_bnve = sem("s_bnve")
        s_bnrs = sem("s_bnrs")
        s_wxn = sem("s_wxn")
        s_zero = sem("s_zero")
        s_pre = [sem(f"s_pre{c}") for c in range(CHAINS)]
        s_y = [sem(f"s_y{c}") for c in range(CHAINS)]
        s_yT = sem("s_yT")
        s_fin = sem("s_fin")
        s_stored = sem("s_stored")
        s_worst = sem("s_worst")
        s_votes = sem("s_votes")
        s_flag = sem("s_flag")
        s_mm = sem("s_mm")
        s_state = sem("s_state")
        s_kept = sem("s_kept")

        def toks(dram):
            return dram.rearrange("(g r) (h q) w c -> r (q w) g h c", g=G, h=HALVES)

        def rep4(dram):
            rows = dram.partition_broadcast(G)
            return rows.rearrange("g a b -> (g a) b") if len(dram.shape) == 2 else rows

        def slab(r):
            return slice(r * G * HALVES, (r + 1) * G * HALVES)

        def step_by_step(engine):
            engine.wait_ge(s_flag, 1)
            return engine.If(engine.value_load(again[0:1, 0:1], min_val=0, max_val=P) > 0)

        block = ctx.enter_context(nc.Block())

        @block.sync
        def _(sp):
            for r in range(R):
                for g in range(G):
                    src = x[g * R + r].rearrange("(h q) w c -> (q w) h c", h=HALVES)
                    sp.dma_start(x_tok[:, r, :, g], src).then_inc(s_x[r], 16)
            for g in range(G):
                sp.dma_start(small4[C * g:C * (g + 1), 3, :], w_ffn).then_inc(s_small, 16)
                sp.dma_start(small4[C * g:C * (g + 1), 4, :], v_ffn).then_inc(s_small, 16)
            def store(time):
                for r in range(R):
                    sp.wait_ge(s_fin, time * R + r + 1)
                    for g in range(G):
                        dst = out[g * R + r].rearrange("(h q) w c -> (q w) h c", h=HALVES)
                        sp.dma_start(dst, out_tok[:, r, :, g]).then_inc(s_stored, 16)

            store(0)
            with step_by_step(sp):
                store(1)
                sp.wait_ge(s_stored, 2 * 16 * R * G)
            sp.wait_ge(s_stored, 16 * R * G)

        @block.gpsimd
        def _(pool):
            count = [0]

            def link(ins):
                count[0] += 1
                ins.then_inc(s_pool, 1)
                pool.wait_ge(s_pool, count[0])

            def select(t, op, fill, base, pattern, mult=1):
                return pool.affine_select(out=t, in_=t, compare_op=op, fill=fill, base=base,
                                          pattern=pattern, channel_multiplier=mult)

            link(pool.memset(ident[:], 0.0))
            select(ident[:], ALU.not_equal, 1.0, 0, [[-1, P]]).then_inc(s_ident, 1)
            link(pool.memset(halfneg[:], -0.5))
            pool.wait_ge(s_ident, 1)
            link(pool.tensor_copy(ident_b[:], ident[:]))
            link(pool.tensor_scalar(negid_b[:], ident[:], -1.0, None, ALU.mult))
            link(pool.memset(blockmask[:], 1.0))
            link(select(blockmask[:], ALU.is_ge, 0.0, 0, [[-C, HEADS], [0, C]]))
            link(select(blockmask[:], ALU.is_ge, 0.0, C - 1, [[C, HEADS], [0, C]], -1))
            link(pool.memset(sel32[:], 0.0))
            link(select(sel32[:], ALU.not_equal, 1.0, 0, [[-HEADS, 8], [-1, HEADS], [0, C]]))
            link(pool.memset(sel4[:], 0.0))
            link(select(sel4[:], ALU.not_equal, 1.0, 0, [[-1, G], [0, P]]))
            link(pool.memset(xn1[:], 1.0))
            for t in (qshift, kshift, sshift):
                link(pool.memset(t[:], 0.0))
            for c in range(HEADS):
                link(pool.tensor_copy(ctxo[:, c, :, P:P + HEADS],
                                      blockmask[:, :, 0:1].rearrange("p h o -> p o h").broadcast_to([P, G, HEADS])))
            pool.nop().then_inc(s_const, 1) if False else link(pool.memset(ones_f[:], 1.0))
            pool.memset(proj[:], 0.0).then_inc(s_const, 1)

            def gn(r):
                pool.wait_ge(s_gnve, r + 1)
                pool.tensor_tensor(gn_rs[:, r:r + 1], gn_ve[:, r:r + 1], halfneg[:, 0:1], ALU.pow).then_inc(s_gnrs, 1)

            def gn_cast(r):
                pool.wait_ge(s_xnT, r + 1)
                pool.tensor_copy(xnT_b[:, r], xnT[:, r]).then_inc(s_xnTb, 1)

            for r in range(R):
                gn(r)
                if r:
                    gn_cast(r - 1)
            gn_cast(R - 1)
            link(pool.memset(sel8[:], 0.0))
            link(select(sel8[:], ALU.not_equal, 1.0, 0, [[-1, 8], [0, P]]))
            link(pool.memset(mask_ts[:], 0.0))
            link(select(mask_ts[:], ALU.is_ge, MASKED, 0, [[-1, P]]))
            link(pool.memset(mask_st[:], 0.0))
            link(select(mask_st[:], ALU.is_ge, MASKED, 0, [[1, P]], -1))
            link(pool.memset(groupavg[:], 0.0))
            for g in range(G):
                link(select(groupavg[:], ALU.not_equal, 1.0 / G, -C * g, [[0, G], [-1, C]]))
            link(pool.memset(v1[:], 1.0))
            pool.memset(warm[:], 0.0).then_inc(s_const, 1)
            pool.wait_ge(s_lnp, 32)
            for r in range(R):
                pool.wait_ge(s_x[r], 16 * G)
                pool.tensor_tensor(xb[:, r], x_tok[:, r].rearrange("p h g c -> p (h g) c"),
                                   bln_bc[:, None, :].broadcast_to([P, 8, C]), ALU.add).then_inc(s_xb, 1)

            def heads(r):
                pool.wait_ge(s_z4, G * (r + 1))
                link(pool.tensor_tensor(z4[:, r, :, 0:2 * C], z4[:, r, :, 0:2 * C], z4[:, r, :, 2 * C:4 * C], ALU.add))
                pool.tensor_tensor(z[:, r], z4[:, r, :, 0:C], z4[:, r, :, C:2 * C], ALU.add).then_inc(s_z, 1)
                pool.wait_ge(s_z, r + 1)
                pool.tensor_tensor(zg[:, r], z[:, r], gln_bc[:, None, :].broadcast_to([P, 8, C]),
                                   ALU.mult).then_inc(s_zg, 1)

            def power(n, r):
                pool.wait_ge(s_ve[n], r + 1)
                pool.tensor_tensor(ln_rs[:, n, r], ln_ve[:, n, r], halfneg[:], ALU.pow).then_inc(s_rs[n], 1)

            def cast(src, dst, ready, done, r):
                pool.wait_ge(ready, r + 1)
                pool.tensor_copy(dst[:, r], src[:, r]).then_inc(done, 1)

            for r in range(R):
                heads(r)
                power(0, r)
                power(1, r)
            for r in range(R + 1):
                if r < R:
                    cast(tnT, tnT_b, s_tnT, s_tnTb, r)
                    cast(uT, uT_b, s_uT, s_uTb, r)
                if r >= 1:
                    power(2, r - 1)
            pool.wait_ge(s_bnve, 1)
            pool.tensor_tensor(bn_sc[:, 1:2], bn_sc[:, 0:1], halfneg[:, 0:1], ALU.pow).then_inc(s_bnrs, 1)
            pool.memset(state[:, :, 0:STRIDE - 1], 0.0).then_inc(s_kept, 1)
            with step_by_step(pool):
                with pool.Fori(0, CHUNKS) as j:
                    pool.wait_ge(s_state, (j + 1) * STRIDE + 1)
                    pool.tensor_copy(ys[:, :, bass.ds(j, 1), :], state[:, :, None, :]).then_inc(s_kept, 1)

        @block.scalar
        def _(act):
            for g in range(G):
                act.dma_start(wqkv4[C * g:C * (g + 1), :], w_qkv).then_inc(s_wqkv, 16)
            act.dma_start(wout_sb[:], w_out).then_inc(s_wout, 16)
            act.dma_start(brow[C:C + 1, :], b_out.rearrange("(a c) -> a c", a=1)).then_inc(s_wout, 16)
            for g in range(G):
                for n, w in enumerate((w_q, w_k, w_v)):
                    act.dma_start(small4[C * g:C * (g + 1), n, :], w).then_inc(s_small, 16)
            act.dma_start(gln_bc[:], g_ln.partition_broadcast(P)).then_inc(s_lnp, 16)
            act.dma_start(bln_bc[:], b_ln.partition_broadcast(P)).then_inc(s_lnp, 16)
            for g in range(G):
                act.dma_start(gam4[C * g:C * (g + 1), :], gamma.rearrange("(c a) -> c a", a=1)).then_inc(s_small, 16)
                act.dma_start(bet4[C * g:C * (g + 1), :], beta.rearrange("(c a) -> c a", a=1)).then_inc(s_small, 16)

            def evac(dst, src, ready, n, done):
                act.wait_ge(ready, n)
                act.copy(dst, src).then_inc(done, 1)

            for r in range(R):
                act.wait_ge(s_const, 1)
                evac(xn1[:, r, :, :, 0:C], bank[4 + r][:, 0:256].rearrange("p (h g c) -> p h g c", h=2, g=G),
                     s_xnk, r + 1, s_xn1)

            def exp_a(r):
                for g in range(G):
                    act.wait_ge(s_qk, r * G + g + 1)
                    act.activation(eqk[:, r, g], bank[g][:], ACT.Exp).then_inc(s_expA, 1)

            def square(n, src, r):
                act.wait_ge(s_sqin[n], r + 1)
                act.activation(sq[:, n, r], src[:, r], ACT.Square).then_inc(s_sq[n], 1)

            def square_z(r):
                act.wait_ge(s_z, r + 1)
                act.activation(sq[:, 0, r], z[:, r], ACT.Square).then_inc(s_sq[0], 1)

            for r in range(R + 1):
                if r < R:
                    exp_a(r)
                    evac(gram[:, r], bank[4][0:C + 1, :], s_gram, r + 1, s_gramS)
                if r >= 1:
                    square_z(r - 1)
                    square(1, tc[:, 0], r - 1)

            def project(r):
                evac(tnT[:, r], bank[4][:, 0:TW], s_T, r + 1, s_tnT)
                evac(uT[:, r], bank[5][:, 0:TW], s_u, r + 1, s_uT)
                evac(v1[:, r, :, :, 0:C], bank[6][:, 0:256].rearrange("p (h g c) -> p h g c", h=2, g=G),
                     s_v, r + 1, s_v1)

            def exp_b(r):
                for g in range(G):
                    act.wait_ge(s_st, r * G + g + 1)
                    act.activation(probsT[:, r, g], bank[g][:, 0:3 * P], ACT.Exp).then_inc(s_expB, 1)

            def finish(r):
                square(2, tc[:, 1], r)
                evac(tn2T[:, r], bank[4][:, 0:TW], s_T2, r + 1, s_tn2T)
                evac(wxT[:, r], bank[5][:, 0:TW], s_wx, r + 1, s_wxS)

            project(0)
            for r in range(R):
                if r + 1 < R:
                    project(r + 1)
                exp_b(r)
                if r >= 1:
                    finish(r - 1)
            finish(R - 1)

            for s in range(STEPS):
                j0 = max(0, LEAD - s // STRIDE)
                for c in range(CHAINS):
                    rr = slice(c * RPC, (c + 1) * RPC)
                    dst = warm[:, s, rr, j0:] if s < WARM else ys[:, rr, :, s - WARM]
                    if s == 0:
                        act.wait_ge(s_wxn, STRIDE)
                        src = wxn[:, 0, rr, 0:CHUNKS - j0]
                    else:
                        act.wait_ge(s_pre[c], s)
                        src = bank[2 * c + s % 2][:, 0:RPC * CHUNKS].rearrange("p (r j) -> p r j", r=RPC)[:, :, j0:]
                    if s == 0 and c == 0:
                        act.wait_ge(s_const, 2)
                    act.activation(dst, src, ACT.Sigmoid).then_inc(s_y[c], 1)
            with step_by_step(act):
                with act.Fori(0, CHUNKS) as j:
                    act.wait_ge(s_kept, j + 1)
                    for m in range(STRIDE):
                        act.wait_ge(s_mm, j * STRIDE + (m + 1))
                        act.activation(state[:, :, m], bank[m][:, 0:R], ACT.Sigmoid).then_inc(s_state, 1)

        @block.vector
        def _(dve):
            count = [0]

            def link(ins):
                count[0] += 1
                ins.then_inc(s_dve, 1)
                dve.wait_ge(s_dve, count[0])

            dve.wait_ge(s_wqkv, 16 * G)
            dve.tensor_copy(wqk4_b[:], wqkv4[:, 0:2 * P]).then_inc(s_wqkb, 1)
            for r in range(R):
                dve.wait_ge(s_xT, r + 1)
                link(dve.bn_stats(gn_stats[:, r], bank[4 + r][:, 0:TW]))
                link(dve.bn_aggr(gn_mv[:, r], gn_stats[:, r]))
                dve.tensor_scalar(gn_ve[:, r:r + 1], gn_mv[:, r, 1:2], EPS, None, ALU.add).then_inc(s_gnve, 1)
            for r in range(R):
                dve.wait_ge(s_gnrs, r + 1)
                dve.tensor_scalar(xnT[:, r], bank[4 + r][:, 0:TW], gn_mv[:, r, 0:1], gn_rs[:, r:r + 1],
                                  ALU.subtract, ALU.mult).then_inc(s_xnT, 1)

            dve.wait_ge(s_const, 1)
            dve.wait_ge(s_wout, 32)
            link(dve.tensor_reduce(wout_sum[:], wout_sb[:], AX_X, ALU.add))
            link(dve.tensor_scalar(wout_sum[:], wout_sum[:], 1.0 / C, None, ALU.mult))
            link(dve.tensor_scalar(wout_c[:], wout_sb[:], wout_sum[:, 0:1], ATTN_SCALE, ALU.subtract, ALU.mult))
            link(dve.tensor_reduce(bsum[C:C + 1, :], brow[C:C + 1, :], AX_X, ALU.add))
            link(dve.tensor_scalar(bsum[C:C + 1, :], bsum[C:C + 1, :], 1.0 / C, None, ALU.mult))
            link(dve.tensor_scalar(proj[C:C + 1, 0:C], brow[C:C + 1, :], bsum[C:C + 1, 0:1], None, ALU.subtract))
            link(dve.memset(proj[C:C + 1, P:P + 1], 1.0))
            dve.tensor_tensor(wout_bd[:], wout_c[:, None, :].broadcast_to([P, HEADS, C]), blockmask[:],
                              ALU.mult).then_inc(s_wprep, 1)
            dve.wait_ge(s_wpe, 1)
            dve.tensor_copy(wv_t[:], bank[0][:, 0:C]).then_inc(s_wev, 1)
            dve.wait_ge(s_wpe, 2)
            dve.tensor_copy(proj[0:C, 0:P], bank[1][0:C, 0:P]).then_inc(s_wev, 1)
            dve.wait_ge(s_small, 16 * 7 * G)
            for n in range(5):
                ins = dve.tensor_tensor(small_bd[:, n], small4[:, n, None, :].broadcast_to([P, G, C]), blockmask[:],
                                        ALU.mult)
            ins.then_inc(s_wprep, 1)
            dve.wait_ge(s_wpe, 3)
            dve.tensor_scalar(score_bd[:], bank[2][:, 0:P], ATTN_SCALE, None, ALU.mult)
            dve.tensor_copy(wvT_bd[:], bank[2][:, P:2 * P])
            dve.tensor_copy(wT_bd[:], bank[2][:, 2 * P:3 * P])
            dve.tensor_copy(vT_bd[:], bank[2][:, 3 * P:4 * P]).then_inc(s_wev, 1)

            def max_a(r):
                for g in range(G):
                    dve.wait_ge(s_maxA, r * G + g + 1)
                    dve.tensor_reduce(qmax_b[:, r, :, g, :],
                                      bank[g][:, 0:256].rearrange("p (h e d) -> p h e d", h=2, d=C), AX_X, ALU.max)
                    dve.tensor_reduce(kmax_b[:, r, g:g + 1], bank[g][:, 256:512], AX_X, ALU.max).then_inc(s_redA, 1)
                dve.wait_ge(s_negA, r + 1)
                dve.tensor_copy(qshift[0:32, r], bank[6][0:32, 0:P])
                dve.tensor_copy(kshift[0:G, r], bank[6][0:G, P:2 * P]).then_inc(s_shA, 1)

            def contexts(r):
                for half in range(2):
                    dve.wait_ge(s_ctx, 2 * r + half + 1)
                    m = bank[5 + half][:, 0:272].rearrange("p (g n) -> p g n", g=2)
                    link(dve.reciprocal(ksum_r[:, r, 2 * half:2 * half + 2], m[:, :, P]))
                    for i in range(2):
                        ins = dve.scalar_tensor_tensor(
                            out=ctxo[:, r, 2 * half + i, 0:P], in0=m[:, i, 0:P],
                            scalar=ksum_r[:, r, 2 * half + i:2 * half + i + 1],
                            in1=blockmask[:].rearrange("p h c -> p (h c)"), op0=ALU.mult, op1=ALU.mult)
                    ins.then_inc(s_ctxS, 1)

            def heads(r):
                for g in range(G):
                    dve.wait_ge(s_out, r * G + g + 1)
                    o = bank[(7, 4)[g % 2]][:, 0:264].rearrange("p (h n) -> p h n", h=2)
                    rq = qsum_r[:, r, g].rearrange("p (h e) -> p h e", h=2)
                    link(dve.reciprocal(rq, o[:, :, P:P + HEADS]))
                    for h in range(2):
                        ins = dve.tensor_tensor(z4[:, r, h * G + g].rearrange("p (e c) -> p e c", e=HEADS),
                                                o[:, h, 0:P].rearrange("p (e c) -> p e c", e=HEADS),
                                                rq[:, h, :, None].broadcast_to([P, HEADS, C]), ALU.mult)
                    ins.then_inc(s_z4, 1)

            def bc(t):
                return t[:, :, None].broadcast_to([P, G * HALVES, C])

            def variance(n, r):
                dve.wait_ge(s_sq[n], r + 1)
                link(dve.tensor_reduce(ln_sum[:, n, r], sq[:, n, r], AX_X, ALU.add))
                dve.tensor_scalar(ln_ve[:, n, r], ln_sum[:, n, r], 1.0 / C, EPS, ALU.mult, ALU.add).then_inc(s_ve[n], 1)

            def center(n, src, r):
                link(dve.tensor_reduce(ln_mean[:, n, r], src[:, r], AX_X, ALU.add))
                link(dve.tensor_scalar(ln_mean[:, n, r], ln_mean[:, n, r], 1.0 / C, None, ALU.mult))
                dve.tensor_tensor(tc[:, n - 1, r], src[:, r], bc(ln_mean[:, n, r]), ALU.subtract).then_inc(s_sqin[n], 1)

            def normalize(n, r):
                dve.wait_ge(s_rs[n], r + 1)
                dve.tensor_tensor(tn[:, n - 1, r].rearrange("p h g c -> p (h g) c"), tc[:, n - 1, r],
                                  bc(ln_rs[:, n, r]), ALU.mult).then_inc(s_tn[n - 1], 1)

            def norm_a(r):
                variance(0, r)
                dve.wait_ge(s_rs[0], r + 1)
                dve.wait_ge(s_zg, r + 1)
                link(dve.tensor_tensor(zg[:, r], zg[:, r], bc(ln_rs[:, 0, r]), ALU.mult))
                dve.wait_ge(s_xb, r + 1)
                link(dve.tensor_tensor(t1[:, r], zg[:, r], xb[:, r], ALU.add))
                center(1, t1, r)
                variance(1, r)
                normalize(1, r)

            max_a(0)
            for r in range(R):
                contexts(r)
                heads(r)
                if r + 1 < R:
                    max_a(r + 1)
                norm_a(r)

            def max_b(r):
                for g in range(G):
                    dve.wait_ge(s_maxB, r * G + g + 1)
                    dve.tensor_reduce(smax_b[:, r, 0, g:g + 1], bank[g][:, 0:P], AX_X, ALU.max)
                    dve.tensor_reduce(smax_b[:, r, 1, g:g + 1], bank[g][:, P:3 * P], AX_X, ALU.max).then_inc(s_redB, 1)
                dve.wait_ge(s_negB, r + 1)
                dve.tensor_copy(sshift[0:8, r], bank[4][0:8, 0:P]).then_inc(s_shB, 1)

            def attend(r):
                dve.wait_ge(s_pv, r + 1)
                pv = bank[7][:, 0:264].rearrange("p (k n) -> p k n", n=C + 1)
                link(dve.reciprocal(psum_r[:, r], pv[:, :, C]))
                dve.tensor_tensor(attn[:, r], pv[:, :, 0:C], bc(psum_r[:, r]), ALU.mult).then_inc(s_attn, 1)
                dve.wait_ge(s_attn, r + 1)
                link(dve.tensor_tensor(t2[:, r], attn[:, r], t1[:, r], ALU.add))
                center(2, t2, r)
                variance(2, r)
                normalize(2, r)

            def wx_stats(r):
                dve.wait_ge(s_wxS, r + 1)
                link(dve.bn_stats(bn_stats[:, r], wxT[:, r]))

            max_b(0)
            for r in range(R):
                if r + 1 < R:
                    max_b(r + 1)
                attend(r)
                if r >= 1:
                    wx_stats(r - 1)
            wx_stats(R - 1)

            link(dve.bn_aggr(bn_mv[:], bn_stats[:].rearrange("p r n -> p (r n)")))
            link(dve.tensor_copy(bn_in[:, 0:1], bn_mv[:, 0:1]))
            dve.scalar_tensor_tensor(out=bn_in[:, 1:2], in0=bn_mv[:, 0:1], scalar=bn_mv[:, 0:1], in1=bn_mv[:, 1:2],
                                     op0=ALU.mult, op1=ALU.add).then_inc(s_bnin, 1)
            dve.wait_ge(s_bnp, 1)
            link(dve.tensor_copy(bn_tot[:], bank[6][:, 0:2]))
            link(dve.tensor_tensor(bn_sc[:, 2:3], bn_tot[:, 0:1], bn_tot[:, 0:1], ALU.mult))
            link(dve.tensor_tensor(bn_sc[:, 3:4], bn_tot[:, 1:2], bn_sc[:, 2:3], ALU.subtract))
            dve.tensor_scalar(bn_sc[:, 0:1], bn_sc[:, 3:4], EPS, None, ALU.add).then_inc(s_bnve, 1)
            dve.wait_ge(s_bnrs, 1)
            link(dve.tensor_tensor(bn_sc[:, 4:5], bn_sc[:, 1:2], gam4[:], ALU.mult))
            link(dve.tensor_tensor(bn_sc[:, 5:6], bn_tot[:, 0:1], bn_sc[:, 4:5], ALU.mult))
            link(dve.tensor_tensor(bn_sc[:, 6:7], bet4[:], bn_sc[:, 5:6], ALU.subtract))
            for m in range(STRIDE):
                dve.tensor_scalar(wxn[:, m], wxT[:].rearrange("p r (j m) -> p m r j", m=STRIDE)[:, m],
                                  bn_sc[:, 4:5], bn_sc[:, 6:7], ALU.mult, ALU.add).then_inc(s_wxn, 1)

            def residual(time):
                for r in range(R):
                    dve.wait_ge(s_yT, time * R + r + 1)
                    dve.tensor_tensor(
                        out_tok[:, r].rearrange("p h g c -> p (h g c)"), bank[4 + r][:, 0:TW],
                        t2[:, r].rearrange("p k c -> p (k c)"), ALU.add).then_inc(s_fin, 1)

            dve.memset(state[:, :, STRIDE - 1:], 0.0).then_inc(s_state, 1)
            for c in range(CHAINS):
                dve.wait_ge(s_y[c], STEPS)
            link(dve.tensor_tensor(diff[:], warm[:, WARM - 1, :, 1:], ys[:, :, 0:CHUNKS - 1, STRIDE - 1], ALU.subtract))
            link(dve.tensor_tensor(diff[:], diff[:], diff[:], ALU.mult))
            link(dve.tensor_reduce(worst[:, 0:1], diff[:].rearrange("p r j -> p (r j)"), AX_X, ALU.max))
            dve.tensor_scalar(worst[:, 1:2], worst[:, 0:1], AGREE ** 2, None, ALU.is_gt).then_inc(s_worst, 1)
            residual(0)
            dve.wait_ge(s_votes, 1)
            dve.tensor_copy(again[:], bank[0][0:1, 0:1]).then_inc(s_flag, 1)
            with step_by_step(dve):
                dve.wait_ge(s_stored, 16 * R * G)
                residual(1)

        @block.tensor
        def _(pe):
            def rows(t, g):
                return t[C * g:C * (g + 1)]

            pe.wait_ge(s_ident, 1)
            for r in range(R):
                pe.wait_ge(s_x[r], 16 * G)
                for h in range(HALVES):
                    ins = pe.transpose(bank[4 + r][:, h * P:(h + 1) * P], x_tok[:, r, h].rearrange("p g c -> p (g c)"), ident[:])
                ins.then_inc(s_xT, 1)
            for r in range(R):
                pe.wait_ge(s_xnT, r + 1)
                for h in range(HALVES):
                    ins = pe.transpose(bank[4 + r][:, h * P:(h + 1) * P], xnT[:, r, h * P:(h + 1) * P], ident[:])
                ins.then_inc(s_xnk, 1)
            pe.transpose(bank[0][:, 0:C], wqkv4[0:C, 2 * P:3 * P], ident[0:C, 0:C]).then_inc(s_wpe, 1)
            pe.wait_ge(s_wev, 1)
            pe.wait_ge(s_wprep, 1)
            pe.matmul(bank[1][0:C, 0:P], wv_t[:], wout_bd[:].rearrange("p h c -> p (h c)"),
                      start=True, stop=True).then_inc(s_wpe, 1)
            pe.wait_ge(s_wprep, 2)
            bd = [small_bd[:, n].rearrange("p g c -> p (g c)") for n in range(5)]
            pe.matmul(bank[2][:, 0:P], bd[0], bd[1], start=True, stop=True)
            for n in range(3):
                ins = pe.transpose(bank[2][:, (n + 1) * P:(n + 2) * P], bd[2 + n], ident[:])
            ins.then_inc(s_wpe, 1)

            def max_a(r):
                if r == 0:
                    pe.wait_ge(s_wqkb, 1)
                    pe.wait_ge(s_wev, 3)
                else:
                    pe.wait_ge(s_expA, r * G)
                pe.wait_ge(s_xnTb, r + 1)
                for h in range(HALVES):
                    for g in range(G):
                        pe.matmul(bank[g][:, h * P:(h + 1) * P], rows(xnT_b, g)[:, r, h * P:(h + 1) * P],
                                  rows(wqk4_b, g)[:, 0:P], start=True, stop=True)
                for g in range(G):
                    pe.matmul(bank[g][:, 256:512], rows(wqk4_b, g)[:, P:2 * P], rows(xnT_b, g)[:, r, :],
                              start=True, stop=True).then_inc(s_maxA, 1)

            def neg_a(r):
                if r == 0:
                    pe.wait_ge(s_xn1, R)
                pe.wait_ge(s_redA, G * (r + 1))
                pe.matmul(bank[6][0:32, 0:P], qmax_b[:, r].rearrange("p h g e -> p (h g e)"), negid_b[:],
                          start=True, stop=True)
                pe.matmul(bank[6][0:G, P:2 * P], kmax_b[:, r], negid_b[:], start=True, stop=True).then_inc(s_negA, 1)

            def qk(r):
                for g in range(G):
                    pe.matmul(bank[g][:, 0:256], rows(wqkv4, g)[:, 0:P], rows(xnT, g)[:, r, :],
                              start=True, stop=True)
                for h in range(HALVES):
                    for g in range(G):
                        pe.matmul(bank[g][:, 256 + h * P:256 + (h + 1) * P], rows(xnT, g)[:, r, h * P:(h + 1) * P],
                                  rows(wqkv4, g)[:, P:2 * P], start=False, stop=True, skip_group_check=True)
                pe.wait_ge(s_shA, r + 1)
                for g in range(G):
                    for h in range(HALVES):
                        pe.matmul(bank[g][:, h * P:(h + 1) * P], sel32[:, h * G + g, :], qshift[:, r],
                                  start=False, stop=True, skip_group_check=True)
                    for h in range(HALVES):
                        ins = pe.matmul(bank[g][:, 256 + h * P:256 + (h + 1) * P], sel4[:, g, :], kshift[:, r],
                                        start=False, stop=True, skip_group_check=True)
                    ins.then_inc(s_qk, 1)

            def grams(r):
                if r:
                    pe.wait_ge(s_z4, G * r)
                for g in range(G):
                    pe.wait_ge(s_expA, r * G + g + 1)
                    for h in range(HALVES):
                        ins = pe.matmul(bank[4][0:C + 1, g * P:(g + 1) * P], xn1[:, r, h, g, :],
                                        eqk[:, r, g, 256 + h * P:256 + (h + 1) * P], start=(h == 0), stop=(h == 1))
                ins.then_inc(s_gram, 1)

            def contexts(r):
                pe.wait_ge(s_gramS, r + 1)
                for g in range(G):
                    ins = pe.matmul(bank[5 + g // 2][:, 136 * (g % 2):136 * (g % 2) + P + 1],
                                    gram[:, r, g * P:(g + 1) * P], proj[:], start=True, stop=True)
                    if g % 2:
                        ins.then_inc(s_ctx, 1)

            def outs(r):
                for g in range(G):
                    pe.wait_ge(s_ctxS, 2 * r + g // 2 + 1)
                    if r * G + g >= 2:
                        pe.wait_ge(s_z4, r * G + g - 1)
                    for h in range(HALVES):
                        ins = pe.matmul(bank[(7, 4)[g % 2]][:, h * 132:(h + 1) * 132], eqk[:, r, g, h * P:(h + 1) * P],
                                        ctxo[:, r, g, :], start=True, stop=True)
                    ins.then_inc(s_out, 1)

            max_a(0)
            neg_a(0)
            for r in range(R):
                qk(r)
                grams(r)
                contexts(r)
                outs(r)
                if r + 1 < R:
                    max_a(r + 1)
                    neg_a(r + 1)

            def project(r):
                if r == 0:
                    pe.wait_ge(s_const, 2)
                    pe.wait_ge(s_z4, G * R)
                pe.wait_ge(s_tn[0], r + 1)
                for h in range(HALVES):
                    ins = pe.transpose(bank[4][:, h * P:(h + 1) * P], tn[:, 0, r, h].rearrange("p g c -> p (g c)"), ident[:])
                ins.then_inc(s_T, 1)
                pe.wait_ge(s_tnT, r + 1)
                if r >= 3:
                    pe.wait_ge(s_wxS, r - 2)
                pe.matmul(bank[5][:, 0:TW], score_bd[:], tnT[:, r], start=True, stop=True).then_inc(s_u, 1)
                if r:
                    pe.wait_ge(s_v1, r)
                for h in range(HALVES):
                    ins = pe.matmul(bank[6][:, h * P:(h + 1) * P], tnT[:, r, h * P:(h + 1) * P], wvT_bd[:],
                                    start=True, stop=True)
                ins.then_inc(s_v, 1)

            def max_b(r):
                pe.wait_ge(s_tnTb, r + 1)
                pe.wait_ge(s_uTb, r + 1)
                if r:
                    pe.wait_ge(s_expB, r * G)
                else:
                    pe.wait_ge(s_expA, R * G)
                for h in range(HALVES):
                    for g in range(G):
                        pe.matmul(bank[g][:, h * P:h * P + (h + 1) * P], rows(uT_b, g)[:, r, h * P:(h + 1) * P],
                                  rows(tnT_b, g)[:, r, 0:(h + 1) * P], start=(h == 0), stop=True,
                                  skip_group_check=(h == 1))
                for g in range(G):
                    for h in range(HALVES):
                        ins = pe.matmul(bank[g][:, 2 * h * P:(2 * h + 1) * P], ident_b[:], mask_ts[:],
                                        start=False, stop=True, skip_group_check=True)
                    ins.then_inc(s_maxB, 1)

            def neg_b(r):
                pe.wait_ge(s_redB, G * (r + 1))
                pe.matmul(bank[4][0:8, 0:P], smax_b[:, r].rearrange("p h g -> p (h g)"), negid_b[:],
                          start=True, stop=True).then_inc(s_negB, 1)

            def scores(r):
                pe.wait_ge(s_redB, G * (r + 1))
                for ks in range(HALVES):
                    for g in range(G):
                        pe.matmul(bank[g][:, 256 * ks:256 * ks + TW - ks * P], rows(tnT, g)[:, r, ks * P:(ks + 1) * P],
                                  rows(uT, g)[:, r, ks * P:TW], start=(ks == 0), stop=True,
                                  skip_group_check=(ks == 1))
                pe.wait_ge(s_shB, r + 1)
                for g in range(G):
                    for ks in range(HALVES):
                        pe.matmul(bank[g][:, 256 * ks:256 * ks + P], ident_b[:], mask_st[:],
                                  start=False, stop=True, skip_group_check=True)
                        for qs in range(ks, HALVES):
                            at = 256 * ks + (qs - ks) * P
                            ins = pe.matmul(bank[g][:, at:at + P], sel8[:, qs * G + g, :], sshift[:, r],
                                            start=False, stop=True, skip_group_check=True)
                    ins.then_inc(s_st, 1)

            def values(r):
                if r:
                    pe.wait_ge(s_attn, r)
                pe.wait_ge(s_v1, r + 1)
                for g in range(G):
                    pe.wait_ge(s_expB, r * G + g + 1)
                    for qs in range(HALVES):
                        k = qs * G + g
                        o = bank[7][:, k * (C + 1):(k + 1) * (C + 1)]
                        for ks in range(qs + 1):
                            at = 256 * ks + (qs - ks) * P
                            ins = pe.matmul(o, probsT[:, r, g, at:at + P], v1[:, r, ks, g, :],
                                            start=(ks == 0), stop=(ks == qs))
                ins.then_inc(s_pv, 1)

            def ffn(r):
                pe.wait_ge(s_tn[1], r + 1)
                for h in range(HALVES):
                    ins = pe.transpose(bank[4][:, h * P:(h + 1) * P], tn[:, 1, r, h].rearrange("p g c -> p (g c)"), ident[:])
                ins.then_inc(s_T2, 1)
                pe.wait_ge(s_tn2T, r + 1)
                pe.wait_ge(s_uT, min(r + 3, R))
                pe.matmul(bank[5][:, 0:TW], wT_bd[:], tn2T[:, r], start=True, stop=True).then_inc(s_wx, 1)

            project(0)
            for r in range(R):
                max_b(r)
                if r >= 1:
                    values(r - 1)
                if r + 1 < R:
                    project(r + 1)
                neg_b(r)
                scores(r)
                if r >= 1:
                    ffn(r - 1)
            values(R - 1)
            ffn(R - 1)

            pe.wait_ge(s_bnin, 1)
            pe.matmul(bank[6][:, 0:2], groupavg[:].rearrange("p g c -> p (g c)"), bn_in[:],
                      start=True, stop=True).then_inc(s_bnp, 1)

            def part(c, s):
                return bank[2 * c + s % 2][:, 0:RPC * CHUNKS].rearrange("p (r j) -> p r j", r=RPC)

            def inputs(c, s):
                j0 = max(0, LEAD - s // STRIDE)
                if s >= 3:
                    pe.wait_ge(s_y[c], s - 1)
                at = s // STRIDE - LEAD
                pe.matmul(part(c, s)[:, :, j0:], ident[:], wxn[:, s % STRIDE, c * RPC:(c + 1) * RPC, j0 + at:CHUNKS + at],
                          start=True, stop=False)

            pe.wait_ge(s_wxn, STRIDE)
            for c in range(CHAINS):
                inputs(c, 1)
            for s in range(1, STEPS):
                j0 = max(0, LEAD - s // STRIDE)
                for c in range(CHAINS):
                    pe.wait_ge(s_y[c], s)
                    rr = slice(c * RPC, (c + 1) * RPC)
                    src = warm[:, s - 1, rr, j0:] if s <= WARM else ys[:, rr, :, s - 1 - WARM]
                    pe.matmul(part(c, s)[:, :, j0:], vT_bd[:], src, start=False, stop=True).then_inc(s_pre[c], 1)
                    if s + 1 < STEPS:
                        inputs(c, s + 1)

            def back(time):
                for r in range(R):
                    if time:
                        pe.wait_ge(s_fin, R)
                    else:
                        pe.wait_ge(s_y[r // RPC], STEPS)
                    for h in range(HALVES):
                        js = slice(h * CHUNKS // 2, (h + 1) * CHUNKS // 2)
                        ins = pe.transpose(bank[4 + r][:, h * P:(h + 1) * P],
                                           ys[:, r, js].rearrange("p j m -> p (j m)"), ident[:])
                    ins.then_inc(s_yT, 1)

            back(0)
            pe.wait_ge(s_worst, 1)
            pe.matmul(bank[0][0:1, 0:1], worst[:, 1:2], ones_f[:], start=True, stop=True).then_inc(s_votes, 1)
            with step_by_step(pe):
                with pe.Fori(0, CHUNKS) as j:
                    for m in range(STRIDE):
                        pe.matmul(bank[m][:, 0:R], ident[:], wxn[:, m, :, bass.ds(j, 1)], start=True, stop=False)
                        pe.wait_ge(s_state, j * STRIDE + (m + 1))
                        pe.matmul(bank[m][:, 0:R], vT_bd[:], state[:, :, (m + STRIDE - 1) % STRIDE],
                                  start=False, stop=True).then_inc(s_mm, 1)
                pe.wait_ge(s_kept, CHUNKS + 1)
                back(1)


_INS = ["x", "L0_conv_w_qkv", "L0_conv_w_out", "L0_conv_b_out", "L0_conv_g_ln", "L0_conv_b_ln", "L1_attn_Wq",
        "L1_attn_Wk", "L1_attn_Wv", "L1_ffn_W", "L1_ffn_V", "L1_ffn_gamma", "L1_ffn_beta"]


def kernel(**inputs):
    import concourse.bacc as _bacc
    from concourse.bass_utils import run_bass_kernel_spmd as _run

    nc = _bacc.Bacc("TRN2", target_bir_lowering=False, num_devices=1)
    arrays, args = {}, []
    for name in _INS:
        a = np.ascontiguousarray(inputs[name])
        arrays[f"in_{name}_dram"] = a
        args.append(nc.dram_tensor(f"in_{name}_dram", a.shape, mybir.dt.from_np(a.dtype), kind="ExternalInput").ap())
    shape = np.asarray(inputs["x"]).shape
    args.append(nc.dram_tensor("out_0_dram", shape, F32, kind="ExternalOutput").ap())
    conv_attn_rnn(nc, *args)
    r = _run(nc, [arrays], core_ids=[0])
    return r.results[0]["out_0_dram"]
```

```python
from contextlib import ExitStack

import numpy as np

import concourse.bass as bass
from concourse import mybir

ALU = mybir.AluOpType
ACT = mybir.ActivationFunctionType
F32 = mybir.dt.float32
BF16 = mybir.dt.bfloat16
I32 = mybir.dt.int32
AX_X = mybir.AxisListType.X

P = 128


def conv_attn_rnn(nc, x, w_qkv, w_out, b_out, g_ln, b_ln, w_q, w_k, w_v, w_ffn, v_ffn, gamma, beta, out):
    B, HH, WW, C = x.shape
    T = HH * WW
    G = P // C
    R = B // G
    HALVES = T // P
    HEADS = w_out.shape[0] // C
    TW = HALVES * P
    RC = G * HALVES * C
    ATTN_SCALE = float(C) ** -0.5
    MASKED = -1e30
    EPS = 1e-5
    assert (P, G, R, HALVES, HEADS) == (128, 4, 4, 2, 4)

    STRIDE = 4
    CHUNKS = T // STRIDE
    WARM = 12
    LEAD = WARM // STRIDE
    STEPS = WARM + STRIDE
    CHAINS = 2
    RPC = R // CHAINS
    AGREE = 2.0 ** -20

    with ExitStack() as ctx:
        def sb(name, shape, dt=F32):
            return ctx.enter_context(nc.sbuf_tensor(name, shape, dt))

        def sem(name):
            return ctx.enter_context(nc.semaphore(name))

        bank = [ctx.enter_context(nc.psum_tensor(f"bank{i}", [P, 512], F32)) for i in range(8)]

        x_tok = sb("x_tok", [P, R, HALVES, G, C])
        wqkv4 = sb("wqkv4", [P, 3 * P])
        wqk4_b = sb("wqk4_b", [P, 2 * P], BF16)
        wout_sb = sb("wout_sb", [P, C])
        wout_sum = sb("wout_sum", [P, 1])
        wout_c = sb("wout_c", [P, C])
        wout_bd = sb("wout_bd", [P, HEADS, C])
        wv_t = sb("wv_t", [P, C])
        proj = sb("proj", [C + 1, P + 1])
        brow = sb("brow", [C + 1, C])
        bsum = sb("bsum", [C + 1, 1])
        gln_bc = sb("gln_bc", [P, C])
        bln_bc = sb("bln_bc", [P, C])
        w_raw = sb("w_raw", [C, 3 * P + 5 * C + 2])
        small4 = sb("small4", [P, 5 * C + 2])
        gam4 = small4[:, 5 * C:5 * C + 1]
        bet4 = small4[:, 5 * C + 1:5 * C + 2]
        small_bd = sb("small_bd", [P, 5, G, C])
        wvT_bd = sb("wvT_bd", [P, P])
        wT_bd = sb("wT_bd", [P, P])
        vT_bd = sb("vT_bd", [P, P])
        score_bd = sb("score_bd", [P, P])

        ident = sb("ident", [P, P])
        ident_b = sb("ident_b", [P, P], BF16)
        rep_id = sb("rep_id", [C, G, C])
        negid_b = sb("negid_b", [P, P], BF16)
        blockmask = sb("blockmask", [P, HEADS, C])
        groupavg = sb("groupavg", [P, G, C])
        ones_f = sb("ones_f", [P, 1])
        halfneg = sb("halfneg", [P, 8])
        sel32 = sb("sel32", [P, 8, P], BF16)
        sel4 = sb("sel4", [P, G, P], BF16)
        sel8 = sb("sel8", [P, 8, P], BF16)
        mask_ts = sb("mask_ts", [P, P], BF16)
        mask_st = sb("mask_st", [P, P], BF16)

        gn_stats = sb("gn_stats", [P, R, 6])
        gn_mv = sb("gn_mv", [P, R, 2])
        gn_ve = sb("gn_ve", [P, R])
        gn_rs = sb("gn_rs", [P, R])
        xnT = sb("xnT", [P, R, TW])
        xnT_b = sb("xnT_b", [P, R, TW], BF16)
        xn1 = sb("xn1", [P, R, HALVES, G, C + 1])
        xb = sb("xb", [P, R, G * HALVES, C])

        qmax_b = sb("qmax_b", [P, R, HALVES, G, HEADS], BF16)
        kmax_b = sb("kmax_b", [P, R, G], BF16)
        qshift = sb("qshift", [P, R, P], BF16)
        kshift = sb("kshift", [P, R, P], BF16)
        eqk = sb("eqk", [P, R, G, 512])
        gram = sb("gram", [C + 1, R, G * P])
        ksum_r = sb("ksum_r", [P, R, G])
        ctxo = sb("ctxo", [P, R, G, P + HEADS])
        qsum_r = sb("qsum_r", [P, R, G, HALVES * HEADS])
        z4 = sb("z4", [P, R, G * HALVES, HEADS * C])
        z = sb("z", [P, R, G * HALVES, C])
        zg = sb("zg", [P, R, G * HALVES, C])

        sq = sb("sq", [P, 3, R, G * HALVES, C])
        ln_sum = sb("ln_sum", [P, 3, R, G * HALVES])
        ln_mean = sb("ln_mean", [P, 3, R, G * HALVES])
        ln_ve = sb("ln_ve", [P, 3, R, G * HALVES])
        ln_rs = sb("ln_rs", [P, 3, R, G * HALVES])
        t1 = sb("t1", [P, R, G * HALVES, C])
        tc = sb("tc", [P, 2, R, G * HALVES, C])
        tn = sb("tn", [P, 2, R, HALVES, G, C])

        tnT = sb("tnT", [P, R, TW])
        tnT_b = sb("tnT_b", [P, R, TW], BF16)
        uT = sb("uT", [P, R, TW])
        uT_b = sb("uT_b", [P, R, TW], BF16)
        v1 = sb("v1", [P, R, HALVES, G, C + 1])
        smax_b = sb("smax_b", [P, R, HALVES, G], BF16)
        sshift = sb("sshift", [P, R, P], BF16)
        probsT = eqk[:, :, :, 0:3 * P]
        psum_r = sb("psum_r", [P, R, G * HALVES])
        attn = sb("attn", [P, R, G * HALVES, C])
        t2 = sb("t2", [P, R, G * HALVES, C])
        tn2T = sb("tn2T", [P, R, TW])
        wxT = sb("wxT", [P, R, TW])

        bn_stats = sb("bn_stats", [P, R, 6])
        bn_mv = sb("bn_mv", [P, 2])
        bn_in = sb("bn_in", [P, 2])
        bn_tot = sb("bn_tot", [P, 2])
        bn_sc = sb("bn_sc", [P, 8])
        wxn = sb("wxn", [P, STRIDE, R, CHUNKS])
        ys = sb("ys", [P, R, CHUNKS, STRIDE])
        warm = sb("warm", [P, WARM, R, CHUNKS])
        out_tok = sb("out_tok", [P, R, HALVES, G, C])
        diff = sb("diff", [P, R, CHUNKS - 1])
        worst = sb("worst", [P, 2])
        again = sb("again", [1, 1], I32)
        state = sb("state", [P, R, STRIDE])

        s_x = [sem(f"s_x{r}") for r in range(R)]
        s_wraw = sem("s_wraw")
        s_rep = sem("s_rep")
        s_wqkv4 = sem("s_wqkv4")
        s_small4 = sem("s_small4")
        s_wout = sem("s_wout")
        s_lnp = sem("s_lnp")
        s_ident = sem("s_ident")
        s_rows = sem("s_rows")
        s_const = sem("s_const")
        s_pool = sem("s_pool")
        s_dve = sem("s_dve")
        s_xT = sem("s_xT")
        s_gnve = sem("s_gnve")
        s_gnrs = sem("s_gnrs")
        s_xnT = sem("s_xnT")
        s_xnTb = sem("s_xnTb")
        s_xnk = sem("s_xnk")
        s_xn1 = sem("s_xn1")
        s_xb = sem("s_xb")
        s_wqkb = sem("s_wqkb")
        s_wprep = sem("s_wprep")
        s_wpe = sem("s_wpe")
        s_wev = sem("s_wev")
        s_maxA = sem("s_maxA")
        s_redA = sem("s_redA")
        s_negA = sem("s_negA")
        s_shA = sem("s_shA")
        s_qk = sem("s_qk")
        s_expA = sem("s_expA")
        s_gram = sem("s_gram")
        s_gramS = sem("s_gramS")
        s_ctx = sem("s_ctx")
        s_ctxS = sem("s_ctxS")
        s_out = sem("s_out")
        s_z4 = sem("s_z4")
        s_z = sem("s_z")
        s_zg = sem("s_zg")
        s_sqin = [sem(f"s_sqin{n}") for n in range(3)]
        s_sq = [sem(f"s_sq{n}") for n in range(3)]
        s_ve = [sem(f"s_ve{n}") for n in range(3)]
        s_rs = [sem(f"s_rs{n}") for n in range(3)]
        s_tn = [sem(f"s_tn{n}") for n in range(2)]
        s_T = sem("s_T")
        s_tnT = sem("s_tnT")
        s_tnTb = sem("s_tnTb")
        s_u = sem("s_u")
        s_uT = sem("s_uT")
        s_uTb = sem("s_uTb")
        s_v1 = sem("s_v1")
        s_maxB = sem("s_maxB")
        s_redB = sem("s_redB")
        s_negB = sem("s_negB")
        s_shB = sem("s_shB")
        s_st = sem("s_st")
        s_expB = sem("s_expB")
        s_pv = sem("s_pv")
        s_attn = sem("s_attn")
        s_T2 = sem("s_T2")
        s_tn2T = sem("s_tn2T")
        s_wx = sem("s_wx")
        s_wxS = sem("s_wxS")
        s_bnin = sem("s_bnin")
        s_bnp = sem("s_bnp")
        s_bnve = sem("s_bnve")
        s_bnrs = sem("s_bnrs")
        s_wxn = sem("s_wxn")
        s_zero = sem("s_zero")
        s_pre = [sem(f"s_pre{c}") for c in range(CHAINS)]
        s_y = [sem(f"s_y{c}") for c in range(CHAINS)]
        s_yT = sem("s_yT")
        s_fin = sem("s_fin")
        s_stored = sem("s_stored")
        s_worst = sem("s_worst")
        s_votes = sem("s_votes")
        s_flag = sem("s_flag")
        s_mm = sem("s_mm")
        s_state = sem("s_state")
        s_kept = sem("s_kept")

        def batches(dram, r, h):
            rows = dram.rearrange("(g r) (h q) w c -> r h (q w) g c", g=G, h=HALVES)
            return rows[r, h]

        def step_by_step(engine):
            engine.wait_ge(s_flag, 1)
            return engine.If(engine.value_load(again[0:1, 0:1], min_val=0, max_val=P) > 0)

        block = ctx.enter_context(nc.Block())

        @block.sync
        def _(sp):
            for r in range(R):
                for h in range(HALVES):
                    sp.dma_start(x_tok[:, r, h], batches(x, r, h)).then_inc(s_x[r], 16)
            sp.dma_start(wout_sb[:], w_out).then_inc(s_wout, 16)
            sp.dma_start(brow[C:C + 1, :], b_out.rearrange("(a c) -> a c", a=1)).then_inc(s_wout, 16)

            def store(time):
                for r in range(R):
                    sp.wait_ge(s_fin, time * R + r + 1)
                    for h in range(HALVES):
                        sp.dma_start(batches(out, r, h), out_tok[:, r, h]).then_inc(s_stored, 16)

            store(0)
            with step_by_step(sp):
                store(1)
                sp.wait_ge(s_stored, 2 * 16 * R * HALVES)
            sp.wait_ge(s_stored, 16 * R * HALVES)

        @block.gpsimd
        def _(pool):
            count = [0]

            def link(ins):
                count[0] += 1
                ins.then_inc(s_pool, 1)
                pool.wait_ge(s_pool, count[0])

            def select(t, op, fill, base, pattern, mult=1):
                return pool.affine_select(out=t, in_=t, compare_op=op, fill=fill, base=base,
                                          pattern=pattern, channel_multiplier=mult)

            link(pool.memset(ident[:], 0.0))
            select(ident[:], ALU.not_equal, 1.0, 0, [[-1, P]]).then_inc(s_ident, 1)
            link(pool.memset(rep_id[:], 0.0))
            select(rep_id[:], ALU.not_equal, 1.0, 0, [[0, G], [-1, C]]).then_inc(s_ident, 1)
            link(pool.memset(halfneg[:], -0.5))
            link(pool.memset(blockmask[:], 1.0))
            link(select(blockmask[:], ALU.is_ge, 0.0, 0, [[-C, HEADS], [0, C]]))
            select(blockmask[:], ALU.is_ge, 0.0, C - 1, [[C, HEADS], [0, C]], -1).then_inc(s_const, 1)

            def gn(r):
                pool.wait_ge(s_gnve, r + 1)
                pool.tensor_tensor(gn_rs[:, r:r + 1], gn_ve[:, r:r + 1], halfneg[:, 0:1], ALU.pow).then_inc(s_gnrs, 1)

            def gn_cast(r):
                pool.wait_ge(s_xnT, r + 1)
                pool.tensor_copy(xnT_b[:, r], xnT[:, r]).then_inc(s_xnTb, 1)

            link(pool.memset(sel32[:], 0.0))
            gn(0)
            link(select(sel32[:], ALU.not_equal, 1.0, 0, [[-HEADS, 8], [-1, HEADS], [0, C]]))
            gn_cast(0)
            gn(1)
            link(pool.memset(sel4[:], 0.0))
            select(sel4[:], ALU.not_equal, 1.0, 0, [[-1, G], [0, P]]).then_inc(s_const, 1)
            gn_cast(1)
            gn(2)
            gn_cast(2)
            gn(3)
            gn_cast(3)
            pool.wait_ge(s_lnp, 32)
            for r in range(R):
                pool.wait_ge(s_x[r], 16 * HALVES)
                pool.tensor_tensor(xb[:, r], x_tok[:, r].rearrange("p h g c -> p (h g) c"),
                                   bln_bc[:, None, :].broadcast_to([P, 8, C]), ALU.add).then_inc(s_xb, 1)
            link(pool.memset(sel8[:], 0.0))
            link(select(sel8[:], ALU.not_equal, 1.0, 0, [[-1, 8], [0, P]]))
            link(pool.memset(mask_ts[:], 0.0))
            link(select(mask_ts[:], ALU.is_ge, MASKED, 0, [[-1, P]]))
            link(pool.memset(mask_st[:], 0.0))
            link(select(mask_st[:], ALU.is_ge, MASKED, 0, [[1, P]], -1))
            link(pool.memset(groupavg[:], 0.0))
            for g in range(G - 1):
                link(select(groupavg[:], ALU.not_equal, 1.0 / G, -C * g, [[0, G], [-1, C]]))
            select(groupavg[:], ALU.not_equal, 1.0 / G, -C * (G - 1), [[0, G], [-1, C]]).then_inc(s_const, 1)

            def heads(r):
                pool.wait_ge(s_z4, G * (r + 1))
                link(pool.tensor_tensor(z4[:, r, :, 0:2 * C], z4[:, r, :, 0:2 * C], z4[:, r, :, 2 * C:4 * C], ALU.add))
                pool.tensor_tensor(z[:, r], z4[:, r, :, 0:C], z4[:, r, :, C:2 * C], ALU.add).then_inc(s_z, 1)
                pool.wait_ge(s_z, r + 1)
                pool.tensor_tensor(zg[:, r], z[:, r], gln_bc[:, None, :].broadcast_to([P, 8, C]),
                                   ALU.mult).then_inc(s_zg, 1)

            def power(n, r):
                pool.wait_ge(s_ve[n], r + 1)
                pool.tensor_tensor(ln_rs[:, n, r], ln_ve[:, n, r], halfneg[:], ALU.pow).then_inc(s_rs[n], 1)

            def cast(src, dst, ready, done, r):
                pool.wait_ge(ready, r + 1)
                pool.tensor_copy(dst[:, r], src[:, r]).then_inc(done, 1)

            def casts(r):
                cast(tnT, tnT_b, s_tnT, s_tnTb, r)
                cast(uT, uT_b, s_uT, s_uTb, r)

            for r in range(2):
                heads(r)
                power(0, r)
                power(1, r)
            heads(2)
            power(0, 2)
            casts(0)
            casts(1)
            heads(3)
            power(1, 2)
            power(0, 3)
            casts(2)
            power(1, 3)
            power(2, 0)
            casts(3)
            for r in range(1, R):
                power(2, r)
            pool.wait_ge(s_bnve, 1)
            pool.tensor_tensor(bn_sc[:, 1:2], bn_sc[:, 0:1], halfneg[:, 0:1], ALU.pow).then_inc(s_bnrs, 1)
            pool.memset(state[:, :, 0:STRIDE - 1], 0.0).then_inc(s_kept, 1)
            with step_by_step(pool):
                with pool.Fori(0, CHUNKS) as j:
                    pool.wait_ge(s_state, (j + 1) * STRIDE + 1)
                    pool.tensor_copy(ys[:, :, bass.ds(j, 1), :], state[:, :, None, :]).then_inc(s_kept, 1)

        @block.scalar
        def _(act):
            act.dma_start(w_raw[:, 0:3 * P], w_qkv).then_inc(s_wraw, 16)
            for n, w in enumerate((w_q, w_k, w_v, w_ffn, v_ffn)):
                act.dma_start(w_raw[:, 3 * P + n * C:3 * P + (n + 1) * C], w).then_inc(s_wraw, 16)
            for n, w in enumerate((gamma, beta)):
                at = 3 * P + 5 * C + n
                act.dma_start(w_raw[:, at:at + 1], w.rearrange("(c a) -> c a", a=1)).then_inc(s_wraw, 16)
            act.dma_start(gln_bc[:], g_ln.partition_broadcast(P)).then_inc(s_lnp, 16)
            act.dma_start(bln_bc[:], b_ln.partition_broadcast(P)).then_inc(s_lnp, 16)

            def evac(dst, src, ready, n, done):
                act.wait_ge(ready, n)
                act.copy(dst, src).then_inc(done, 1)

            evac(wqkv4[:], bank[0][:, 0:3 * P], s_rep, 1, s_wqkv4)
            evac(small4[:], bank[1][:, 0:5 * C + 2], s_rep, 2, s_small4)
            for r in range(R):
                evac(xn1[:, r, :, :, 0:C], bank[4 + r][:, 0:256].rearrange("p (h g c) -> p h g c", h=2, g=G),
                     s_xnk, r + 1, s_xn1)

            def exp_a(r):
                for g in range(G):
                    act.wait_ge(s_qk, r * G + g + 1)
                    act.activation(eqk[:, r, g], bank[g][:], ACT.Exp).then_inc(s_expA, 1)

            def square(n, src, r):
                act.wait_ge(s_sqin[n], r + 1)
                act.activation(sq[:, n, r], src[:, r], ACT.Square).then_inc(s_sq[n], 1)

            def square_z(r):
                act.wait_ge(s_z, r + 1)
                act.activation(sq[:, 0, r], z[:, r], ACT.Square).then_inc(s_sq[0], 1)

            def gram_out(r):
                evac(gram[:, r], bank[4][0:C + 1, :], s_gram, r + 1, s_gramS)

            def project(r):
                evac(tnT[:, r], bank[5][:, 0:TW], s_T, r + 1, s_tnT)
                evac(uT[:, r], bank[6][:, 0:TW], s_u, r + 1, s_uT)
                evac(v1[:, r, :, :, 0:C], bank[6][:, 256:512].rearrange("p (h g c) -> p h g c", h=2, g=G),
                     s_u, r + 1, s_v1)

            def exp_b(r):
                for g in range(G):
                    act.wait_ge(s_st, r * G + g + 1)
                    act.activation(probsT[:, r, g], bank[g][:, 0:3 * P], ACT.Exp).then_inc(s_expB, 1)

            def finish(r):
                evac(tn2T[:, r], bank[4][:, 0:TW], s_T2, r + 1, s_tn2T)
                evac(wxT[:, r], bank[4][:, 0:TW], s_wx, r + 1, s_wxS)

            def square_1(r):
                square(1, tc[:, 0], r)

            def square_2(r):
                square(2, tc[:, 1], r)

            exp_a(0)
            gram_out(0)
            for r in range(1, R):
                exp_a(r)
                square_z(r - 1)
                if r == R - 1:
                    project(0)
                    project(1)
                gram_out(r)
                if r < R - 1:
                    square_1(r - 1)
            square_z(3)
            square_1(2)
            exp_b(0)
            project(2)
            square_1(3)
            exp_b(1)
            square_2(0)
            project(3)
            exp_b(2)
            square_2(1)
            finish(0)
            exp_b(3)
            square_2(2)
            finish(1)
            square_2(3)
            finish(2)
            finish(3)

            for s in range(STEPS):
                j0 = max(0, LEAD - s // STRIDE)
                for c in range(CHAINS):
                    rr = slice(c * RPC, (c + 1) * RPC)
                    dst = warm[:, s, rr, j0:] if s < WARM else ys[:, rr, :, s - WARM]
                    if s == 0:
                        act.wait_ge(s_wxn, 1)
                        src = wxn[:, 0, rr, 0:CHUNKS - j0]
                    else:
                        act.wait_ge(s_pre[c], s)
                        src = bank[2 * c + s % 2][:, 0:RPC * CHUNKS].rearrange("p (r j) -> p r j", r=RPC)[:, :, j0:]
                    if s == 0 and c == 0:
                        act.wait_ge(s_rows, 2)
                    act.activation(dst, src, ACT.Sigmoid).then_inc(s_y[c], 1)
            with step_by_step(act):
                with act.Fori(0, CHUNKS) as j:
                    act.wait_ge(s_kept, j + 1)
                    for m in range(STRIDE):
                        act.wait_ge(s_mm, j * STRIDE + (m + 1))
                        act.activation(state[:, :, m], bank[m][:, 0:R], ACT.Sigmoid).then_inc(s_state, 1)

        @block.vector
        def _(dve):
            count = [0]

            def link(ins):
                count[0] += 1
                ins.then_inc(s_dve, 1)
                dve.wait_ge(s_dve, count[0])

            dve.memset(qshift[:], 0.0)
            dve.memset(kshift[:], 0.0)
            dve.memset(sshift[:], 0.0)
            dve.memset(ones_f[:], 1.0)
            dve.memset(xn1[:, :, :, :, C:], 1.0)
            dve.memset(proj[:], 0.0).then_inc(s_rows, 1)
            dve.wait_ge(s_rows, 1)
            dve.wait_ge(s_ident, 1)
            dve.tensor_copy(ident_b[:], ident[:])
            link(dve.tensor_scalar(negid_b[:], ident[:], -1.0, None, ALU.mult))

            def gn_stats_of(r):
                dve.wait_ge(s_xT, r + 1)
                link(dve.bn_stats(gn_stats[:, r], bank[4 + r][:, 0:TW]))
                link(dve.bn_aggr(gn_mv[:, r], gn_stats[:, r]))
                dve.tensor_scalar(gn_ve[:, r:r + 1], gn_mv[:, r, 1:2], EPS, None, ALU.add).then_inc(s_gnve, 1)

            def gn_apply(r):
                dve.wait_ge(s_gnrs, r + 1)
                dve.tensor_scalar(xnT[:, r], bank[4 + r][:, 0:TW], gn_mv[:, r, 0:1], gn_rs[:, r:r + 1],
                                  ALU.subtract, ALU.mult).then_inc(s_xnT, 1)

            gn_stats_of(0)
            dve.wait_ge(s_wqkv4, 1)
            dve.tensor_copy(wqk4_b[:], wqkv4[:, 0:2 * P]).then_inc(s_wqkb, 1)
            gn_stats_of(1)
            gn_apply(0)
            gn_stats_of(2)
            gn_apply(1)
            gn_stats_of(3)
            gn_apply(2)
            gn_apply(3)

            def weights():
                dve.wait_ge(s_const, 1)
                dve.wait_ge(s_wout, 32)
                for b in range(G):
                    dve.tensor_copy(ctxo[:, b, :, P:P + HEADS],
                                    blockmask[:, :, 0:1].rearrange("p h o -> p o h").broadcast_to([P, G, HEADS]))
                link(dve.tensor_reduce(wout_sum[:], wout_sb[:], AX_X, ALU.add))
                link(dve.tensor_scalar(wout_sum[:], wout_sum[:], 1.0 / C, None, ALU.mult))
                link(dve.tensor_scalar(wout_c[:], wout_sb[:], wout_sum[:, 0:1], ATTN_SCALE, ALU.subtract, ALU.mult))
                dve.tensor_tensor(wout_bd[:], wout_c[:, None, :].broadcast_to([P, HEADS, C]), blockmask[:],
                                  ALU.mult).then_inc(s_wprep, 1)
                dve.wait_ge(s_wpe, 1)
                dve.tensor_copy(wv_t[:], bank[2][:, 0:C]).then_inc(s_wev, 1)
                dve.wait_ge(s_small4, 1)
                dve.tensor_tensor(small_bd[:], small4[:, 0:5 * C].rearrange("p (n c) -> p n c", n=5)[:, :, None, :]
                                  .broadcast_to([P, 5, G, C]), blockmask[:, None].broadcast_to([P, 5, G, C]),
                                  ALU.mult).then_inc(s_wprep, 1)
                link(dve.tensor_reduce(bsum[C:C + 1, :], brow[C:C + 1, :], AX_X, ALU.add))
                link(dve.tensor_scalar(bsum[C:C + 1, :], bsum[C:C + 1, :], 1.0 / C, None, ALU.mult))
                link(dve.tensor_scalar(proj[C:C + 1, 0:C], brow[C:C + 1, :], bsum[C:C + 1, 0:1], None, ALU.subtract))
                link(dve.memset(proj[C:C + 1, P:P + 1], 1.0))
                dve.wait_ge(s_wpe, 2)
                dve.tensor_copy(proj[0:C, 0:P], bank[3][0:C, 0:P]).then_inc(s_wev, 1)
                dve.wait_ge(s_wpe, 3)
                dve.tensor_scalar(score_bd[:], bank[2][:, 0:P], ATTN_SCALE, None, ALU.mult)
                dve.tensor_copy(wvT_bd[:], bank[2][:, P:2 * P])
                dve.tensor_copy(wT_bd[:], bank[2][:, 2 * P:3 * P])
                dve.tensor_copy(vT_bd[:], bank[2][:, 3 * P:4 * P]).then_inc(s_wev, 1)
                dve.memset(v1[:, :, :, :, C:], 1.0)
                dve.memset(warm[:, :, :, 0:LEAD], 0.0).then_inc(s_rows, 1)

            def max_a(r):
                for g in range(G):
                    dve.wait_ge(s_maxA, r * G + g + 1)
                    dve.tensor_reduce(qmax_b[:, r, :, g, :],
                                      bank[g][:, 0:256].rearrange("p (h e d) -> p h e d", h=2, d=C), AX_X, ALU.max)
                    dve.tensor_reduce(kmax_b[:, r, g:g + 1], bank[g][:, 256:512], AX_X, ALU.max).then_inc(s_redA, 1)

            def shift_a(r):
                dve.wait_ge(s_negA, r + 1)
                dve.tensor_copy(qshift[0:32, r], bank[7][0:32, 0:P])
                dve.tensor_copy(kshift[0:G, r], bank[7][0:G, P:2 * P]).then_inc(s_shA, 1)

            def contexts(r):
                m = [bank[5 + half][:, 0:272].rearrange("p (g n) -> p g n", g=2) for half in range(2)]
                for half in range(2):
                    dve.wait_ge(s_ctx, 2 * r + half + 1)
                    ins = dve.reciprocal(ksum_r[:, r, 2 * half:2 * half + 2], m[half][:, :, P])
                link(ins)
                for g in range(G):
                    ins = dve.scalar_tensor_tensor(
                        out=ctxo[:, r, g, 0:P], in0=m[g // 2][:, g % 2, 0:P], scalar=ksum_r[:, r, g:g + 1],
                        in1=blockmask[:].rearrange("p h c -> p (h c)"), op0=ALU.mult, op1=ALU.mult)
                    if g % 2:
                        ins.then_inc(s_ctxS, 1)

            def heads(r):
                for g in range(G):
                    dve.wait_ge(s_out, r * G + g + 1)
                    o = bank[(7, 4)[g % 2]][:, 0:264].rearrange("p (h n) -> p h n", h=2)
                    rq = qsum_r[:, r, g].rearrange("p (h e) -> p h e", h=2)
                    link(dve.reciprocal(rq, o[:, :, P:P + HEADS]))
                    dve.tensor_tensor(z4[:, r].rearrange("p (h g) (e c) -> p g h e c", h=2, e=HEADS)[:, g],
                                      o[:, :, 0:P].rearrange("p h (e c) -> p h e c", e=HEADS),
                                      rq[:, :, :, None].broadcast_to([P, 2, HEADS, C]), ALU.mult).then_inc(s_z4, 1)

            def bc(t):
                return t[:, :, None].broadcast_to([P, G * HALVES, C])

            def variance(n, r):
                dve.wait_ge(s_sq[n], r + 1)
                link(dve.tensor_reduce(ln_sum[:, n, r], sq[:, n, r], AX_X, ALU.add))
                dve.tensor_scalar(ln_ve[:, n, r], ln_sum[:, n, r], 1.0 / C, EPS, ALU.mult, ALU.add).then_inc(s_ve[n], 1)

            def center(n, src, r):
                link(dve.tensor_reduce(ln_mean[:, n, r], src[:, r], AX_X, ALU.add))
                link(dve.tensor_scalar(ln_mean[:, n, r], ln_mean[:, n, r], 1.0 / C, None, ALU.mult))
                dve.tensor_tensor(tc[:, n - 1, r], src[:, r], bc(ln_mean[:, n, r]), ALU.subtract).then_inc(s_sqin[n], 1)

            def normalize(n, r):
                dve.wait_ge(s_rs[n], r + 1)
                dve.tensor_tensor(tn[:, n - 1, r].rearrange("p h g c -> p (h g) c"), tc[:, n - 1, r],
                                  bc(ln_rs[:, n, r]), ALU.mult).then_inc(s_tn[n - 1], 1)

            def gain(r):
                dve.wait_ge(s_rs[0], r + 1)
                dve.wait_ge(s_zg, r + 1)
                link(dve.tensor_tensor(zg[:, r], zg[:, r], bc(ln_rs[:, 0, r]), ALU.mult))
                dve.wait_ge(s_xb, r + 1)
                link(dve.tensor_tensor(t1[:, r], zg[:, r], xb[:, r], ALU.add))
                center(1, t1, r)

            def max_b(r):
                for g in range(G):
                    dve.wait_ge(s_maxB, r * G + g + 1)
                    dve.tensor_reduce(smax_b[:, r, 0, g:g + 1], bank[g][:, 0:P], AX_X, ALU.max)
                    dve.tensor_reduce(smax_b[:, r, 1, g:g + 1], bank[g][:, P:3 * P], AX_X, ALU.max).then_inc(s_redB, 1)

            def shift_b(r):
                dve.wait_ge(s_negB, r + 1)
                dve.tensor_copy(sshift[0:8, r], bank[5][0:8, 0:P]).then_inc(s_shB, 1)

            def attend(r):
                dve.wait_ge(s_pv, r + 1)
                pv = bank[7][:, 0:264].rearrange("p (k n) -> p k n", n=C + 1)
                link(dve.reciprocal(psum_r[:, r], pv[:, :, C]))
                dve.tensor_tensor(attn[:, r], pv[:, :, 0:C], bc(psum_r[:, r]), ALU.mult).then_inc(s_attn, 1)
                dve.wait_ge(s_attn, r + 1)
                link(dve.tensor_tensor(t2[:, r], attn[:, r], t1[:, r], ALU.add))
                center(2, t2, r)

            def wx_stats(r):
                dve.wait_ge(s_wxS, r + 1)
                link(dve.bn_stats(bn_stats[:, r], wxT[:, r]))

            weights()
            max_a(0)
            shift_a(0)
            for r in range(R):
                if r >= 1:
                    heads(r - 1)
                if r >= 2:
                    normalize(1, r - 2)
                if r + 1 < R:
                    max_a(r + 1)
                if r >= 1:
                    variance(0, r - 1)
                if r + 1 < R:
                    shift_a(r + 1)
                contexts(r)
                if 1 <= r < R - 1:
                    gain(r - 1)
                    variance(1, r - 1)
            max_b(0)
            heads(3)
            shift_b(0)
            gain(2)
            variance(1, 2)
            normalize(1, 2)
            max_b(1)
            variance(0, 3)
            shift_b(1)
            gain(3)
            variance(1, 3)
            normalize(1, 3)
            for r in range(R):
                attend(r)
                if r + 2 < R:
                    max_b(r + 2)
                variance(2, r)
                if r + 2 < R:
                    shift_b(r + 2)
                normalize(2, r)
                if r >= 1:
                    wx_stats(r - 1)
            wx_stats(R - 1)

            link(dve.bn_aggr(bn_mv[:], bn_stats[:].rearrange("p r n -> p (r n)")))
            link(dve.tensor_copy(bn_in[:, 0:1], bn_mv[:, 0:1]))
            dve.scalar_tensor_tensor(out=bn_in[:, 1:2], in0=bn_mv[:, 0:1], scalar=bn_mv[:, 0:1], in1=bn_mv[:, 1:2],
                                     op0=ALU.mult, op1=ALU.add).then_inc(s_bnin, 1)
            dve.wait_ge(s_bnp, 1)
            link(dve.tensor_copy(bn_tot[:], bank[6][:, 0:2]))
            link(dve.tensor_tensor(bn_sc[:, 2:3], bn_tot[:, 0:1], bn_tot[:, 0:1], ALU.mult))
            link(dve.tensor_tensor(bn_sc[:, 3:4], bn_tot[:, 1:2], bn_sc[:, 2:3], ALU.subtract))
            dve.tensor_scalar(bn_sc[:, 0:1], bn_sc[:, 3:4], EPS, None, ALU.add).then_inc(s_bnve, 1)
            dve.wait_ge(s_bnrs, 1)
            link(dve.tensor_tensor(bn_sc[:, 4:5], bn_sc[:, 1:2], gam4, ALU.mult))
            link(dve.tensor_tensor(bn_sc[:, 5:6], bn_tot[:, 0:1], bn_sc[:, 4:5], ALU.mult))
            link(dve.tensor_tensor(bn_sc[:, 6:7], bet4, bn_sc[:, 5:6], ALU.subtract))
            for m in range(STRIDE):
                dve.tensor_scalar(wxn[:, m], wxT[:].rearrange("p r (j m) -> p m r j", m=STRIDE)[:, m],
                                  bn_sc[:, 4:5], bn_sc[:, 6:7], ALU.mult, ALU.add).then_inc(s_wxn, 1)

            def residual(time):
                for r in range(R):
                    dve.wait_ge(s_yT, time * R + r + 1)
                    dve.tensor_tensor(
                        out_tok[:, r].rearrange("p h g c -> p (h g c)"), bank[4 + r][:, 0:TW],
                        t2[:, r].rearrange("p k c -> p (k c)"), ALU.add).then_inc(s_fin, 1)

            dve.memset(state[:, :, STRIDE - 1:], 0.0).then_inc(s_state, 1)
            residual(0)
            link(dve.tensor_tensor(diff[:], warm[:, WARM - 1, :, 1:], ys[:, :, 0:CHUNKS - 1, STRIDE - 1], ALU.subtract))
            link(dve.tensor_tensor(diff[:], diff[:], diff[:], ALU.mult))
            link(dve.tensor_reduce(worst[:, 0:1], diff[:].rearrange("p r j -> p (r j)"), AX_X, ALU.max))
            dve.tensor_scalar(worst[:, 1:2], worst[:, 0:1], AGREE ** 2, None, ALU.is_gt).then_inc(s_worst, 1)
            dve.wait_ge(s_votes, 1)
            dve.tensor_copy(again[:], bank[0][0:1, 0:1]).then_inc(s_flag, 1)
            with step_by_step(dve):
                dve.wait_ge(s_stored, 16 * R * HALVES)
                residual(1)

        @block.tensor
        def _(pe):
            def rows(t, g):
                return t[C * g:C * (g + 1)]

            pe.wait_ge(s_ident, 2)
            pe.wait_ge(s_wraw, 16 * 8)
            rep = rep_id[:].rearrange("p g c -> p (g c)")
            pe.matmul(bank[0][:, 0:3 * P], rep, w_raw[:, 0:3 * P], start=True, stop=True).then_inc(s_rep, 1)
            pe.matmul(bank[1][:, 0:5 * C + 2], rep, w_raw[:, 3 * P:], start=True, stop=True).then_inc(s_rep, 1)
            for r in range(R):
                pe.wait_ge(s_x[r], 16 * HALVES)
                for h in range(HALVES):
                    ins = pe.transpose(bank[4 + r][:, h * P:(h + 1) * P], x_tok[:, r, h].rearrange("p g c -> p (g c)"),
                                       ident[:])
                ins.then_inc(s_xT, 1)
            for r in range(R):
                pe.wait_ge(s_xnT, r + 1)
                for h in range(HALVES):
                    ins = pe.transpose(bank[4 + r][:, h * P:(h + 1) * P], xnT[:, r, h * P:(h + 1) * P], ident[:])
                ins.then_inc(s_xnk, 1)
            pe.wait_ge(s_wqkv4, 1)
            pe.transpose(bank[2][:, 0:C], wqkv4[0:C, 2 * P:3 * P], ident[0:C, 0:C]).then_inc(s_wpe, 1)
            pe.wait_ge(s_wev, 1)
            pe.wait_ge(s_wprep, 1)
            pe.matmul(bank[3][0:C, 0:P], wv_t[:], wout_bd[:].rearrange("p h c -> p (h c)"),
                      start=True, stop=True).then_inc(s_wpe, 1)
            pe.wait_ge(s_wprep, 2)
            bd = [small_bd[:, n].rearrange("p g c -> p (g c)") for n in range(5)]
            pe.matmul(bank[2][:, 0:P], bd[0], bd[1], start=True, stop=True)
            for n in range(3):
                ins = pe.transpose(bank[2][:, (n + 1) * P:(n + 2) * P], bd[2 + n], ident[:])
            ins.then_inc(s_wpe, 1)

            def max_a(r):
                if r == 0:
                    pe.wait_ge(s_wqkb, 1)
                    pe.wait_ge(s_small4, 1)
                    pe.wait_ge(s_wev, 3)
                else:
                    pe.wait_ge(s_expA, r * G)
                pe.wait_ge(s_xnTb, r + 1)
                for h in range(HALVES):
                    for g in range(G):
                        pe.matmul(bank[g][:, h * P:(h + 1) * P], rows(xnT_b, g)[:, r, h * P:(h + 1) * P],
                                  rows(wqk4_b, g)[:, 0:P], start=True, stop=True)
                for g in range(G):
                    pe.matmul(bank[g][:, 256:512], rows(wqk4_b, g)[:, P:2 * P], rows(xnT_b, g)[:, r, :],
                              start=True, stop=True).then_inc(s_maxA, 1)

            def neg_a(r):
                if r == 0:
                    pe.wait_ge(s_xn1, R)
                    pe.wait_ge(s_const, 2)
                pe.wait_ge(s_redA, G * (r + 1))
                pe.matmul(bank[7][0:32, 0:P], qmax_b[:, r].rearrange("p h g e -> p (h g e)"), negid_b[:],
                          start=True, stop=True)
                pe.matmul(bank[7][0:G, P:2 * P], kmax_b[:, r], negid_b[:], start=True, stop=True).then_inc(s_negA, 1)

            def queries(r):
                for g in range(G):
                    pe.wait_ge(s_redA, r * G + g + 1)
                    pe.matmul(bank[g][:, 0:256], rows(wqkv4, g)[:, 0:P], rows(xnT, g)[:, r, :],
                              start=True, stop=True)

            def keys(r):
                for h in range(HALVES):
                    for g in range(G):
                        pe.matmul(bank[g][:, 256 + h * P:256 + (h + 1) * P], rows(xnT, g)[:, r, h * P:(h + 1) * P],
                                  rows(wqkv4, g)[:, P:2 * P], start=False, stop=True, skip_group_check=True)

            def shifts_a(r):
                pe.wait_ge(s_shA, r + 1)
                for g in range(G):
                    for h in range(HALVES):
                        pe.matmul(bank[g][:, h * P:(h + 1) * P], sel32[:, h * G + g, :], qshift[:, r],
                                  start=False, stop=True, skip_group_check=True)
                    for h in range(HALVES):
                        ins = pe.matmul(bank[g][:, 256 + h * P:256 + (h + 1) * P], sel4[:, g, :], kshift[:, r],
                                        start=False, stop=True, skip_group_check=True)
                    ins.then_inc(s_qk, 1)

            def grams(r):
                if r:
                    pe.wait_ge(s_z4, G * r)
                for g in range(G):
                    pe.wait_ge(s_expA, r * G + g + 1)
                    for h in range(HALVES):
                        ins = pe.matmul(bank[4][0:C + 1, g * P:(g + 1) * P], xn1[:, r, h, g, :],
                                        eqk[:, r, g, 256 + h * P:256 + (h + 1) * P], start=(h == 0), stop=(h == 1))
                ins.then_inc(s_gram, 1)

            def contexts(r):
                pe.wait_ge(s_gramS, r + 1)
                for g in range(G):
                    ins = pe.matmul(bank[5 + g // 2][:, 136 * (g % 2):136 * (g % 2) + P + 1],
                                    gram[:, r, g * P:(g + 1) * P], proj[:], start=True, stop=True)
                    if g % 2:
                        ins.then_inc(s_ctx, 1)

            def outs(r):
                for g in range(G):
                    pe.wait_ge(s_ctxS, 2 * r + g // 2 + 1)
                    if r * G + g >= 2:
                        pe.wait_ge(s_z4, r * G + g - 1)
                    for h in range(HALVES):
                        ins = pe.matmul(bank[(7, 4)[g % 2]][:, h * 132:(h + 1) * 132], eqk[:, r, g, h * P:(h + 1) * P],
                                        ctxo[:, r, g, :], start=True, stop=True)
                    ins.then_inc(s_out, 1)

            def turn(r):
                if r == 1:
                    pe.wait_ge(s_tnT, 1)
                if r == 2:
                    pe.wait_ge(s_ctxS, 2 * R)
                if r >= 2:
                    pe.wait_ge(s_shB, r - 1)
                pe.wait_ge(s_tn[0], r + 1)
                for h in range(HALVES):
                    ins = pe.transpose(bank[5][:, h * P:(h + 1) * P], tn[:, 0, r, h].rearrange("p g c -> p (g c)"),
                                       ident[:])
                ins.then_inc(s_T, 1)

            def project(r):
                if r:
                    pe.wait_ge(s_v1, r)
                pe.wait_ge(s_tnT, r + 1)
                pe.matmul(bank[6][:, 0:TW], score_bd[:], tnT[:, r], start=True, stop=True)
                for h in range(HALVES):
                    ins = pe.matmul(bank[6][:, 256 + h * P:256 + (h + 1) * P], tnT[:, r, h * P:(h + 1) * P],
                                    wvT_bd[:], start=True, stop=True)
                ins.then_inc(s_u, 1)

            def max_b(r):
                if r == 0:
                    pe.wait_ge(s_const, 3)
                pe.wait_ge(s_tnTb, r + 1)
                pe.wait_ge(s_uTb, r + 1)
                if r:
                    pe.wait_ge(s_expB, r * G)
                else:
                    pe.wait_ge(s_expA, R * G)
                for h in range(HALVES):
                    for g in range(G):
                        pe.matmul(bank[g][:, h * P:h * P + (h + 1) * P], rows(uT_b, g)[:, r, h * P:(h + 1) * P],
                                  rows(tnT_b, g)[:, r, 0:(h + 1) * P], start=(h == 0), stop=True,
                                  skip_group_check=(h == 1))
                for g in range(G):
                    for h in range(HALVES):
                        ins = pe.matmul(bank[g][:, 2 * h * P:(2 * h + 1) * P], ident_b[:], mask_ts[:],
                                        start=False, stop=True, skip_group_check=True)
                    ins.then_inc(s_maxB, 1)

            def neg_b(r):
                pe.wait_ge(s_redB, G * (r + 1))
                pe.matmul(bank[5][0:8, 0:P], smax_b[:, r].rearrange("p h g -> p (h g)"), negid_b[:],
                          start=True, stop=True).then_inc(s_negB, 1)

            def scores(r, ks):
                for g in range(G):
                    pe.wait_ge(s_redB, r * G + g + 1)
                    pe.matmul(bank[g][:, 256 * ks:256 * ks + TW - ks * P], rows(tnT, g)[:, r, ks * P:(ks + 1) * P],
                              rows(uT, g)[:, r, ks * P:TW], start=(ks == 0), stop=True,
                              skip_group_check=(ks == 1))

            def masks(r):
                for g in range(G):
                    for ks in range(HALVES):
                        pe.matmul(bank[g][:, 256 * ks:256 * ks + P], ident_b[:], mask_st[:],
                                  start=False, stop=True, skip_group_check=True)

            def shifts_b(r):
                pe.wait_ge(s_shB, r + 1)
                for g in range(G):
                    for ks in range(HALVES):
                        for qs in range(ks, HALVES):
                            at = 256 * ks + (qs - ks) * P
                            ins = pe.matmul(bank[g][:, at:at + P], sel8[:, qs * G + g, :], sshift[:, r],
                                            start=False, stop=True, skip_group_check=True)
                    ins.then_inc(s_st, 1)

            def values(r):
                if r:
                    pe.wait_ge(s_attn, r)
                else:
                    pe.wait_ge(s_z4, G * R)
                pe.wait_ge(s_v1, r + 1)
                for g in range(G):
                    pe.wait_ge(s_expB, r * G + g + 1)
                    for qs in range(HALVES):
                        k = qs * G + g
                        o = bank[7][:, k * (C + 1):(k + 1) * (C + 1)]
                        for ks in range(qs + 1):
                            at = 256 * ks + (qs - ks) * P
                            ins = pe.matmul(o, probsT[:, r, g, at:at + P], v1[:, r, ks, g, :],
                                            start=(ks == 0), stop=(ks == qs))
                ins.then_inc(s_pv, 1)

            def turn_2(r):
                pe.wait_ge(s_tn[1], r + 1)
                if r:
                    pe.wait_ge(s_wxS, r)
                for h in range(HALVES):
                    ins = pe.transpose(bank[4][:, h * P:(h + 1) * P], tn[:, 1, r, h].rearrange("p g c -> p (g c)"),
                                       ident[:])
                ins.then_inc(s_T2, 1)

            def ffn(r):
                pe.wait_ge(s_tn2T, r + 1)
                pe.matmul(bank[4][:, 0:TW], wT_bd[:], tn2T[:, r], start=True, stop=True).then_inc(s_wx, 1)

            max_a(0)
            queries(0)
            neg_a(0)
            keys(0)
            shifts_a(0)
            for r in range(R):
                if r >= 1:
                    outs(r - 1)
                if r + 1 < R:
                    max_a(r + 1)
                    grams(r)
                    queries(r + 1)
                    neg_a(r + 1)
                    contexts(r)
                    keys(r + 1)
                    shifts_a(r + 1)
            turn(0)
            grams(3)
            project(0)
            turn(1)
            project(1)
            pe.wait_ge(s_v1, 2)
            contexts(3)
            max_b(0)
            outs(3)
            scores(0, 0)
            neg_b(0)
            scores(0, 1)
            masks(0)
            shifts_b(0)
            for r in range(R):
                if r >= 1:
                    values(r - 1)
                if r + 1 < R:
                    max_b(r + 1)
                if r + 2 < R:
                    turn(r + 2)
                if r >= 2:
                    turn_2(r - 2)
                if r + 1 < R:
                    scores(r + 1, 0)
                if r + 2 < R:
                    project(r + 2)
                if r >= 2:
                    ffn(r - 2)
                if r + 1 < R:
                    neg_b(r + 1)
                    scores(r + 1, 1)
                    masks(r + 1)
                    shifts_b(r + 1)
            values(3)
            for r in range(2, R):
                turn_2(r)
                ffn(r)

            pe.wait_ge(s_bnin, 1)
            pe.matmul(bank[6][:, 0:2], groupavg[:].rearrange("p g c -> p (g c)"), bn_in[:],
                      start=True, stop=True).then_inc(s_bnp, 1)

            def part(c, s):
                return bank[2 * c + s % 2][:, 0:RPC * CHUNKS].rearrange("p (r j) -> p r j", r=RPC)

            def inputs(c, s):
                j0 = max(0, LEAD - s // STRIDE)
                if s >= 3:
                    pe.wait_ge(s_y[c], s - 1)
                if s < STRIDE:
                    pe.wait_ge(s_wxn, s + 1)
                at = s // STRIDE - LEAD
                pe.matmul(part(c, s)[:, :, j0:], ident[:], wxn[:, s % STRIDE, c * RPC:(c + 1) * RPC, j0 + at:CHUNKS + at],
                          start=True, stop=False)

            for c in range(CHAINS):
                inputs(c, 1)
            for s in range(1, STEPS):
                j0 = max(0, LEAD - s // STRIDE)
                for c in range(CHAINS):
                    pe.wait_ge(s_y[c], s)
                    rr = slice(c * RPC, (c + 1) * RPC)
                    src = warm[:, s - 1, rr, j0:] if s <= WARM else ys[:, rr, :, s - 1 - WARM]
                    pe.matmul(part(c, s)[:, :, j0:], vT_bd[:], src, start=False, stop=True).then_inc(s_pre[c], 1)
                    if s + 1 < STEPS:
                        inputs(c, s + 1)

            def back(time):
                for r in range(R):
                    if time:
                        pe.wait_ge(s_fin, R)
                    else:
                        pe.wait_ge(s_y[r // RPC], STEPS)
                    for h in range(HALVES):
                        js = slice(h * CHUNKS // 2, (h + 1) * CHUNKS // 2)
                        ins = pe.transpose(bank[4 + r][:, h * P:(h + 1) * P],
                                           ys[:, r, js].rearrange("p j m -> p (j m)"), ident[:])
                    ins.then_inc(s_yT, 1)

            back(0)
            pe.wait_ge(s_worst, 1)
            pe.matmul(bank[0][0:1, 0:1], worst[:, 1:2], ones_f[:], start=True, stop=True).then_inc(s_votes, 1)
            with step_by_step(pe):
                with pe.Fori(0, CHUNKS) as j:
                    for m in range(STRIDE):
                        pe.matmul(bank[m][:, 0:R], ident[:], wxn[:, m, :, bass.ds(j, 1)], start=True, stop=False)
                        pe.wait_ge(s_state, j * STRIDE + (m + 1))
                        pe.matmul(bank[m][:, 0:R], vT_bd[:], state[:, :, (m + STRIDE - 1) % STRIDE],
                                  start=False, stop=True).then_inc(s_mm, 1)
                pe.wait_ge(s_kept, CHUNKS + 1)
                back(1)


_INS = ["x", "L0_conv_w_qkv", "L0_conv_w_out", "L0_conv_b_out", "L0_conv_g_ln", "L0_conv_b_ln", "L1_attn_Wq",
        "L1_attn_Wk", "L1_attn_Wv", "L1_ffn_W", "L1_ffn_V", "L1_ffn_gamma", "L1_ffn_beta"]


def kernel(**inputs):
    import concourse.bacc as _bacc
    from concourse.bass_utils import run_bass_kernel_spmd as _run

    nc = _bacc.Bacc("TRN2", target_bir_lowering=False, num_devices=1)
    arrays, args = {}, []
    for name in _INS:
        a = np.ascontiguousarray(inputs[name])
        arrays[f"in_{name}_dram"] = a
        args.append(nc.dram_tensor(f"in_{name}_dram", a.shape, mybir.dt.from_np(a.dtype), kind="ExternalInput").ap())
    shape = np.asarray(inputs["x"]).shape
    args.append(nc.dram_tensor("out_0_dram", shape, F32, kind="ExternalOutput").ap())
    conv_attn_rnn(nc, *args)
    r = _run(nc, [arrays], core_ids=[0])
    return r.results[0]["out_0_dram"]
```

```python
from contextlib import ExitStack

import numpy as np

import concourse.bass as bass
from concourse import mybir

ALU = mybir.AluOpType
ACT = mybir.ActivationFunctionType
F32 = mybir.dt.float32
BF16 = mybir.dt.bfloat16
I32 = mybir.dt.int32
AX_X = mybir.AxisListType.X

P = 128


def conv_attn_rnn(nc, x, w_qkv, w_out, b_out, g_ln, b_ln, w_q, w_k, w_v, w_ffn, v_ffn, gamma, beta, out):
    B, HH, WW, C = x.shape
    T = HH * WW
    G = P // C
    R = B // G
    HALVES = T // P
    HEADS = w_out.shape[0] // C
    TW = HALVES * P
    TB = G * HALVES
    ATTN_SCALE = float(C) ** -0.5
    MASKED = -1e30
    EPS = 1e-5
    assert (P, G, R, HALVES, HEADS) == (128, 4, 4, 2, 4)

    STRIDE = 4
    CHUNKS = T // STRIDE
    WARM = 12
    LEAD = -(-WARM // STRIDE)
    STEPS = WARM + STRIDE
    CHAINS = 2
    RPC = R // CHAINS
    KEEP = {"inputs": 6, "input 1": 1, "input 2": 2, "value weights": 2,
            "queries 0": 2, "queries 1": 1, "keys 0": 2, "keys 1": 1,
            "projection 1": 3, "weights 0": 3, "turn 2": 3, "projection 2": 2,
            "second turns": 15, "second turn": 3, "batch statistics": 4, "scan": 9}
    AGREE = 2.0 ** -20

    with ExitStack() as ctx:
        def sb(name, shape, dt=F32):
            return ctx.enter_context(nc.sbuf_tensor(name, shape, dt))

        def sem(name):
            return ctx.enter_context(nc.semaphore(name))

        bank = [ctx.enter_context(nc.psum_tensor(f"bank{i}", [P, 512], F32)) for i in range(8)]

        x_tok = sb("x_tok", [P, HALVES, R, G, C])
        wqk4 = sb("wqk4", [P, 2 * P])
        wqk4_b = sb("wqk4_b", [P, 2 * P], BF16)
        wout_sb = sb("wout_sb", [P, C])
        wout_sum = sb("wout_sum", [P, 1])
        wout_c = sb("wout_c", [P, C])
        wout_bd = sb("wout_bd", [P, HEADS, C])
        wv_t = sb("wv_t", [P, C])
        proj = sb("proj", [C + 1, P + 1])
        brow = sb("brow", [C + 1, C])
        bsum = sb("bsum", [C + 1, 1])
        gln_bc = sb("gln_bc", [P, C])
        bln_bc = sb("bln_bc", [P, C])
        w_raw = sb("w_raw", [C, 3 * P + 5 * C + 2])
        small4 = sb("small4", [P, 5 * C + 2])
        gam4 = small4[:, 5 * C:5 * C + 1]
        bet4 = small4[:, 5 * C + 1:5 * C + 2]
        small_bd = sb("small_bd", [P, 5, G, C])
        wvT_bd = sb("wvT_bd", [P, P])
        wT_bd = sb("wT_bd", [P, P])
        vT_bd = sb("vT_bd", [P, P])
        score_bd = sb("score_bd", [P, P])

        table_in = sb("table_in", [P, 1])
        idle_b = sb("idle_b", [P, 512], BF16)
        ident = sb("ident", [P, P])
        ident_b = sb("ident_b", [P, P], BF16)
        rep_id = sb("rep_id", [C, G, C])
        negid_b = sb("negid_b", [P, P], BF16)
        blockmask = sb("blockmask", [P, HEADS, C])
        groupavg = sb("groupavg", [P, G, C])
        ones_f = sb("ones_f", [P, 1])
        halfneg = sb("halfneg", [P, 8])
        sel32 = sb("sel32", [P, 8, P], BF16)
        sel4 = sb("sel4", [P, G, P], BF16)
        sel8 = sb("sel8", [P, 8, P], BF16)
        mask_ts = sb("mask_ts", [P, P], BF16)
        mask_st = sb("mask_st", [P, P], BF16)

        gn_stats = sb("gn_stats", [P, R, 6])
        gn_mv = sb("gn_mv", [P, R, 2])
        gn_ve = sb("gn_ve", [P, R])
        gn_rs = sb("gn_rs", [P, R])
        xnT = sb("xnT", [P, R, TW])
        xnT_b = sb("xnT_b", [P, R, TW], BF16)
        xn1 = sb("xn1", [P, R, HALVES, G, C + 1])
        xb = sb("xb", [P, R, G * HALVES, C])

        qmax_b = sb("qmax_b", [P, R, HALVES, G, HEADS], BF16)
        kmax_b = sb("kmax_b", [P, R, G], BF16)
        qshift = sb("qshift", [P, R, P], BF16)
        kshift = sb("kshift", [P, R, P], BF16)
        eqk = sb("eqk", [P, R, G, 512])
        gram = sb("gram", [C + 1, R, G * P])
        ksum_r = sb("ksum_r", [P, R, G])
        ctxo = sb("ctxo", [P, R, G, P + HEADS])
        qsum_r = sb("qsum_r", [P, R, G, HALVES * HEADS])
        z4 = sb("z4", [P, R, G * HALVES, HEADS * C])
        z = sb("z", [P, R, G * HALVES, C])
        zg = sb("zg", [P, R, G * HALVES, C])

        sq = sb("sq", [P, 2, R, G * HALVES, C])
        ln_sum = sb("ln_sum", [P, 3, R, G * HALVES])
        ln_mean = sb("ln_mean", [P, 3, R, G * HALVES])
        ln_ve = sb("ln_ve", [P, 3, R, G * HALVES])
        ln_rs = sb("ln_rs", [P, 3, R, G * HALVES])
        ln_sd = sb("ln_sd", [P, R, G * HALVES])
        t1 = sb("t1", [P, R, G * HALVES, C])
        tc = sb("tc", [P, 2, R, G * HALVES, C])
        tn = sb("tn", [P, 2, R, HALVES, G, C])

        tnT = sb("tnT", [P, R, TW])
        tnT_b = sb("tnT_b", [P, R, TW], BF16)
        uT = sb("uT", [P, R, TW])
        uT_b = sb("uT_b", [P, R, TW], BF16)
        v1 = sb("v1", [P, R, HALVES, G, 2 * C])
        smax_b = sb("smax_b", [P, R, HALVES, G], BF16)
        sshift = sb("sshift", [P, R, P], BF16)
        probsT = eqk[:, :, :, 0:3 * P]
        pvT = z4[:].rearrange("p r k c -> p r (k c)")[:, :, 0:2 * TW].rearrange("p r (b t) -> p r b t", b=2)
        psum_r = sb("psum_r", [P, R, G * HALVES])
        attn = sb("attn", [P, R, G * HALVES, C])
        t2 = sb("t2", [P, R, G * HALVES, C])
        tn2T = sb("tn2T", [P, R, TW])
        wxT = sb("wxT", [P, R, TW])

        bn_stats = sb("bn_stats", [P, R, 6])
        bn_mv = sb("bn_mv", [P, 2])
        bn_sc = sb("bn_sc", [P, 8])
        wxn = sb("wxn", [P, STRIDE, R, CHUNKS])
        ys = sb("ys", [P, R, CHUNKS, STRIDE])
        warm = sb("warm", [P, WARM, R, CHUNKS])
        out_tok = sb("out_tok", [P, R, G, HALVES, C])
        diff = sb("diff", [P, R, CHUNKS - 1])
        worst = sb("worst", [P, 2])
        again = sb("again", [1, 1], I32)
        state = sb("state", [P, R, STRIDE])

        s_x = [sem(f"s_x{r}") for r in range(R)]
        s_wraw = sem("s_wraw")
        s_wsmall = sem("s_wsmall")
        s_rep = sem("s_rep")
        s_wqk4 = sem("s_wqk4")
        s_small4 = sem("s_small4")
        s_wout = sem("s_wout")
        s_lnp = sem("s_lnp")
        s_ident = sem("s_ident")
        s_idle = sem("s_idle")
        s_rows = sem("s_rows")
        s_const = sem("s_const")
        s_pool = sem("s_pool")
        s_dve = sem("s_dve")
        s_xT = sem("s_xT")
        s_gnve = sem("s_gnve")
        s_gnrs = sem("s_gnrs")
        s_xnT = sem("s_xnT")
        s_xnTb = sem("s_xnTb")
        s_xnk = sem("s_xnk")
        s_xn1 = sem("s_xn1")
        s_xb = sem("s_xb")
        s_wqkb = sem("s_wqkb")
        s_wprep = sem("s_wprep")
        s_wpe = sem("s_wpe")
        s_wev = sem("s_wev")
        s_maxA = sem("s_maxA")
        s_redA = sem("s_redA")
        s_negA = sem("s_negA")
        s_shA = sem("s_shA")
        s_qk = sem("s_qk")
        s_expA = sem("s_expA")
        s_gram = sem("s_gram")
        s_gramS = sem("s_gramS")
        s_ctx = sem("s_ctx")
        s_ctxS = sem("s_ctxS")
        s_out = sem("s_out")
        s_z4 = sem("s_z4")
        s_z = sem("s_z")
        s_t1 = sem("s_t1")
        s_sqin = [sem(f"s_sqin{n}") for n in range(3)]
        s_sq = [sem(f"s_sq{n}") for n in range(3)]
        s_ve = [sem(f"s_ve{n}") for n in range(3)]
        s_rs = [sem(f"s_rs{n}") for n in range(3)]
        s_sd = sem("s_sd")
        s_tn = [sem(f"s_tn{n}") for n in range(2)]
        s_T = sem("s_T")
        s_tnT = sem("s_tnT")
        s_tnTb = sem("s_tnTb")
        s_u = sem("s_u")
        s_uT = sem("s_uT")
        s_uTb = sem("s_uTb")
        s_v1 = sem("s_v1")
        s_maxB = sem("s_maxB")
        s_redB = sem("s_redB")
        s_negB = sem("s_negB")
        s_shB = sem("s_shB")
        s_st = sem("s_st")
        s_expB = sem("s_expB")
        s_pv = sem("s_pv")
        s_pvT = sem("s_pvT")
        s_pvk = sem("s_pvk")
        s_attn = sem("s_attn")
        s_T2 = sem("s_T2")
        s_tn2T = sem("s_tn2T")
        s_wx = sem("s_wx")
        s_wxS = sem("s_wxS")
        s_bnst = sem("s_bnst")
        s_bnin = sem("s_bnin")
        s_bnsc = sem("s_bnsc")
        s_bnp = sem("s_bnp")
        s_bnve = sem("s_bnve")
        s_bnrs = sem("s_bnrs")
        s_wxn = sem("s_wxn")
        s_pre = [sem(f"s_pre{c}") for c in range(CHAINS)]
        s_y = [sem(f"s_y{c}") for c in range(CHAINS)]
        s_yT = sem("s_yT")
        s_fin = sem("s_fin")
        s_stored = sem("s_stored")
        s_worst = sem("s_worst")
        s_votes = sem("s_votes")
        s_flag = sem("s_flag")
        s_mm = sem("s_mm")
        s_state = sem("s_state")
        s_kept = sem("s_kept")

        def place(s):
            at = (s - WARM) // STRIDE
            return (s - WARM) % STRIDE, at, max(0, -at)

        def step_by_step(engine):
            engine.wait_ge(s_flag, 1)
            return engine.If(engine.value_load(again[0:1, 0:1], min_val=0, max_val=P) > 0)

        xbank = [bank[4], bank[5], bank[6], bank[5]]
        assert R == 4

        tbank = [bank[4], bank[5], bank[5], bank[5]]
        vbank = [bank[7], bank[7], bank[7], bank[5]]
        wbank = [bank[4], bank[4], bank[4], bank[7]]

        def neg_banks(r):
            return (bank[7], bank[7]) if r == 0 else (bank[5], bank[5])

        block = ctx.enter_context(nc.Block())

        @block.sync
        def _(sp):
            def load(r):
                for h in range(HALVES):
                    sp.dma_start(x_tok[:, h, r],
                                 x.rearrange("b (h q) w c -> h (q w) b c", h=HALVES)[h, :, G * r:G * (r + 1)])\
                        .then_inc(s_x[r], 16)

            load(0)
            sp.dma_start(w_raw[:, 0:3 * P], w_qkv).then_inc(s_wraw, 16)
            load(1)
            load(2)
            sp.dma_start(wout_sb[:], w_out).then_inc(s_wout, 16)
            sp.dma_start(brow[C:C + 1, :], b_out.rearrange("(a c) -> a c", a=1)).then_inc(s_wout, 16)
            load(3)
            sp.dma_start(gln_bc[:], g_ln.partition_broadcast(P)).then_inc(s_lnp, 16)
            sp.dma_start(bln_bc[:], b_ln.partition_broadcast(P)).then_inc(s_lnp, 16)
            for n, w in enumerate((w_q, w_k, w_v, w_ffn, v_ffn)):
                sp.dma_start(w_raw[:, 3 * P + n * C:3 * P + (n + 1) * C], w).then_inc(s_wsmall, 16)
            for n, w in enumerate((gamma, beta)):
                at = 3 * P + 5 * C + n
                sp.dma_start(w_raw[:, at:at + 1], w.rearrange("(c a) -> c a", a=1)).then_inc(s_wsmall, 16)

            def store(time):
                for r in range(R):
                    sp.wait_ge(s_fin, time * R + r + 1)
                    sp.dma_start(out.rearrange("b (h q) w c -> (q w) (b h) c", h=HALVES)[:, TB * r:TB * (r + 1)],
                                 out_tok[:, r].rearrange("p g h c -> p (g h) c")).then_inc(s_stored, 16)

            store(0)
            with step_by_step(sp):
                store(1)
                sp.wait_ge(s_stored, 2 * 16 * R)
            sp.wait_ge(s_stored, 16 * R)

        @block.gpsimd
        def _(pool):
            count = [0]

            def link(ins):
                count[0] += 1
                ins.then_inc(s_pool, 1)
                pool.wait_ge(s_pool, count[0])

            def select(t, op, fill, base, pattern, mult=1):
                return pool.affine_select(out=t, in_=t, compare_op=op, fill=fill, base=base,
                                          pattern=pattern, channel_multiplier=mult)

            link(pool.memset(ident[:], 0.0))
            select(ident[:], ALU.not_equal, 1.0, 0, [[-1, P]]).then_inc(s_ident, 1)
            link(pool.memset(rep_id[:], 0.0))
            select(rep_id[:], ALU.not_equal, 1.0, 0, [[0, G], [-1, C]]).then_inc(s_ident, 1)
            link(pool.memset(halfneg[:], -0.5))
            link(pool.memset(sel32[:], 0.0))

            def gn(r):
                pool.wait_ge(s_gnve, r + 1)
                pool.tensor_tensor(gn_rs[:, r:r + 1], gn_ve[:, r:r + 1], halfneg[:, 0:1], ALU.pow).then_inc(s_gnrs, 1)

            def gn_cast(r):
                pool.wait_ge(s_xnT, r + 1)
                pool.tensor_copy(xnT_b[:, r], xnT[:, r]).then_inc(s_xnTb, 1)

            gn(0)
            gn(1)
            link(select(sel32[:], ALU.not_equal, 1.0, 0, [[-HEADS, 8], [-1, HEADS], [0, C]]))
            link(pool.memset(sel4[:], 0.0))
            select(sel4[:], ALU.not_equal, 1.0, 0, [[-1, G], [0, P]]).then_inc(s_const, 1)
            gn(2)
            gn_cast(1)
            link(pool.memset(blockmask[:], 1.0))
            link(select(blockmask[:], ALU.is_ge, 0.0, 0, [[-C, HEADS], [0, C]]))
            select(blockmask[:], ALU.is_ge, 0.0, C - 1, [[C, HEADS], [0, C]], -1).then_inc(s_const, 1)
            gn(3)
            gn_cast(2)
            gn_cast(3)
            pool.wait_ge(s_lnp, 32)
            for r in range(R):
                pool.wait_ge(s_x[r], 16 * HALVES)
                pool.tensor_tensor(xb[:, r].rearrange("p (h g) c -> p h g c", h=HALVES), x_tok[:, :, r],
                                   bln_bc[:, None, None, :].broadcast_to([P, HALVES, G, C]), ALU.add).then_inc(s_xb, 1)
            link(pool.memset(sel8[:], 0.0))
            link(select(sel8[:], ALU.not_equal, 1.0, 0, [[-1, 8], [0, P]]))
            link(pool.memset(mask_ts[:], 0.0))
            link(select(mask_ts[:], ALU.is_ge, MASKED, 0, [[-1, P]]))
            link(pool.memset(mask_st[:], 0.0))
            link(select(mask_st[:], ALU.is_ge, MASKED, 0, [[1, P]], -1))
            link(pool.memset(groupavg[:], 0.0))
            for g in range(G - 1):
                link(select(groupavg[:], ALU.not_equal, 1.0 / G, -C * g, [[0, G], [-1, C]]))
            select(groupavg[:], ALU.not_equal, 1.0 / G, -C * (G - 1), [[0, G], [-1, C]]).then_inc(s_const, 1)

            def heads(r):
                pool.wait_ge(s_z4, G * (r + 1))
                link(pool.tensor_tensor(z4[:, r, :, 0:2 * C], z4[:, r, :, 0:2 * C], z4[:, r, :, 2 * C:4 * C], ALU.add))
                pool.tensor_tensor(z[:, r], z4[:, r, :, 0:C], z4[:, r, :, C:2 * C], ALU.add).then_inc(s_z, 1)
                pool.wait_ge(s_z, r + 1)
                link(pool.tensor_tensor(zg[:, r], z[:, r], gln_bc[:, None, :].broadcast_to([P, 8, C]), ALU.mult))

            def power(n, r):
                pool.wait_ge(s_ve[n], r + 1)
                pool.tensor_tensor(ln_rs[:, n, r], ln_ve[:, n, r], halfneg[:], ALU.pow).then_inc(s_rs[n], 1)
                if n == 0:
                    pool.wait_ge(s_rs[0], r + 1)
                    link(pool.tensor_tensor(zg[:, r], zg[:, r],
                                            ln_rs[:, 0, r][:, :, None].broadcast_to([P, G * HALVES, C]), ALU.mult))
                    pool.tensor_tensor(t1[:, r], zg[:, r], xb[:, r], ALU.add).then_inc(s_t1, 1)

            heads(0)
            pool.wait_ge(s_xb, R)
            power(0, 0)
            power(1, 0)
            heads(1)
            power(0, 1)
            heads(2)
            power(1, 1)
            power(0, 2)
            heads(3)
            power(1, 2)
            power(0, 3)
            power(1, 3)
            for r in range(2):
                power(2, r)
            pool.wait_ge(s_bnve, 1)
            pool.tensor_tensor(bn_sc[:, 1:2], bn_sc[:, 0:1], halfneg[:, 0:1], ALU.pow).then_inc(s_bnrs, 1)
            pool.memset(state[:, :, 0:STRIDE - 1], 0.0).then_inc(s_kept, 1)
            with step_by_step(pool):
                with pool.Fori(0, CHUNKS) as j:
                    pool.wait_ge(s_state, (j + 1) * STRIDE + 1)
                    pool.tensor_copy(ys[:, :, bass.ds(j, 1), :], state[:, :, None, :]).then_inc(s_kept, 1)

        @block.scalar
        def _(act):
            def evac(dst, src, ready, n, done):
                act.wait_ge(ready, n)
                act.copy(dst, src).then_inc(done, 1)

            evac(wqk4[:], bank[0][:, 0:2 * P], s_rep, 1, s_wqk4)

            def xn1_out(r):
                evac(xn1[:, r, :, :, 0:C], xbank[r][:, 0:256].rearrange("p (h g c) -> p h g c", h=2, g=G),
                     s_xnk, r + 1, s_xn1)

            def exp_a(r):
                for g in range(G):
                    act.wait_ge(s_qk, r * G + g + 1)
                    act.activation(eqk[:, r, g], bank[g][:], ACT.Exp).then_inc(s_expA, 1)

            def square(n, src, r):
                act.wait_ge(s_sqin[n], r + 1)
                act.activation(sq[:, n % 2, r], src[:, r], ACT.Square).then_inc(s_sq[n], 1)

            def square_z(r):
                act.wait_ge(s_z, r + 1)
                act.activation(sq[:, 0, r], z[:, r], ACT.Square).then_inc(s_sq[0], 1)

            def gram_out(r):
                evac(gram[:, r], bank[4][0:C + 1, :], s_gram, r + 1, s_gramS)

            def turned(r):
                evac(tnT[:, r], tbank[r][:, 0:TW], s_T, r + 1, s_tnT)
                evac(tnT_b[:, r], tbank[r][:, 0:TW], s_T, r + 1, s_tnTb)

            def projected(r):
                evac(uT_b[:, r], bank[6][:, 0:TW], s_u, r + 1, s_uTb)
                evac(uT[:, r], bank[6][:, 0:TW], s_u, r + 1, s_uT)
                evac(v1[:, r, :, :, 0:C], bank[6][:, 256:512].rearrange("p (h g c) -> p h g c", h=2, g=G),
                     s_u, r + 1, s_v1)

            def values_out(r):
                evac(pvT[:, r], vbank[r][:].rearrange("p (b t) -> p b t", b=2), s_pv, 2 * (r + 1), s_pvT)

            def exp_b(r):
                for g in range(G):
                    act.wait_ge(s_st, r * G + g + 1)
                    act.activation(probsT[:, r, g], bank[g][:, 0:3 * P], ACT.Exp).then_inc(s_expB, 1)

            def turned_2(r):
                evac(tn2T[:, r], wbank[r][:, 0:TW], s_T2, r + 1, s_tn2T)

            def ffn_out(r):
                if r == R - 1:
                    act.wait_ge(s_bnst, R)
                evac(wxT[:, r], wbank[r][:, 0:TW], s_wx, r + 1, s_wxS)

            def deviation(r):
                act.wait_ge(s_ve[2], r + 1)
                act.activation(ln_sd[:, r], ln_ve[:, 2, r], ACT.Sqrt).then_inc(s_sd, 1)

            def square_1(r):
                square(1, tc[:, 0], r)

            def square_2(r):
                square(2, tc[:, 1], r)

            for r in range(3):
                xn1_out(r)
            exp_a(0)
            xn1_out(3)
            evac(small4[:], bank[7][:, 0:5 * C + 2], s_rep, 2, s_small4)
            gram_out(0)
            for r in range(1, R):
                exp_a(r)
                if r == R - 1:
                    turned(0)
                if r >= 2:
                    square_z(r - 2)
                if r == R - 1:
                    projected(0)
                gram_out(r)
                if r >= 2:
                    square_1(r - 2)
            square_z(2)
            exp_b(0)
            turned(1)
            projected(1)
            square_1(2)
            square_z(3)
            turned(2)
            exp_b(1)
            projected(2)
            square_1(3)
            values_out(0)
            turned(3)
            square_2(0)
            exp_b(2)
            projected(3)
            values_out(1)
            turned_2(0)
            ffn_out(0)
            square_2(1)
            exp_b(3)
            values_out(2)
            act.activation(table_in[:], ones_f[:], ACT.Sqrt)
            values_out(3)
            turned_2(1)
            ffn_out(1)
            square_2(2)
            deviation(2)
            square_2(3)
            deviation(3)
            turned_2(2)
            ffn_out(2)
            turned_2(3)
            ffn_out(3)
            act.activation(table_in[:], halfneg[:, 0:1], ACT.Sigmoid)

            for s in range(STEPS):
                m, at, j0 = place(s)
                for c in range(CHAINS):
                    rr = slice(c * RPC, (c + 1) * RPC)
                    dst = warm[:, s, rr, j0:] if s < WARM else ys[:, rr, :, s - WARM]
                    if s == 0:
                        if c == 0:
                            act.wait_ge(s_rows, 2)
                        act.wait_ge(s_bnsc, 1)
                        act.wait_ge(s_wxS, R)
                        act.activation(dst, wxT[:, rr].rearrange("p r (j m) -> p m r j", m=STRIDE)[:, m, :, 0:CHUNKS - j0],
                                       ACT.Sigmoid, bias=bn_sc[:, 6:7], scale=bn_sc[:, 4:5]).then_inc(s_y[c], 1)
                        continue
                    else:
                        act.wait_ge(s_pre[c], s)
                        src = bank[2 * c + s % 2][:, 0:RPC * CHUNKS].rearrange("p (r j) -> p r j", r=RPC)[:, :, j0:]
                    act.activation(dst, src, ACT.Sigmoid).then_inc(s_y[c], 1)
            with step_by_step(act):
                with act.Fori(0, CHUNKS) as j:
                    act.wait_ge(s_kept, j + 1)
                    for m in range(STRIDE):
                        act.wait_ge(s_mm, j * STRIDE + (m + 1))
                        act.activation(state[:, :, m], bank[m % 4][:, 0:R], ACT.Sigmoid).then_inc(s_state, 1)

        @block.vector
        def _(dve):
            count = [0]

            def link(ins):
                count[0] += 1
                ins.then_inc(s_dve, 1)
                dve.wait_ge(s_dve, count[0])

            dve.memset(idle_b[:], 1.0).then_inc(s_idle, 1)
            dve.memset(qshift[:], 0.0)
            dve.memset(kshift[:], 0.0)
            dve.memset(sshift[:], 0.0)
            dve.memset(ones_f[:], 1.0)
            dve.memset(xn1[:, :, :, :, C:], 1.0)
            dve.memset(proj[:], 0.0).then_inc(s_rows, 1)
            dve.wait_ge(s_rows, 1)
            dve.wait_ge(s_ident, 1)
            dve.tensor_copy(ident_b[:], ident[:])
            link(dve.tensor_scalar(negid_b[:], ident[:], -1.0, None, ALU.mult))

            def gn_stats_of(r):
                dve.wait_ge(s_xT, r + 1)
                link(dve.bn_stats(gn_stats[:, r], xbank[r][:, 0:TW]))
                link(dve.bn_aggr(gn_mv[:, r], gn_stats[:, r]))
                dve.tensor_scalar(gn_ve[:, r:r + 1], gn_mv[:, r, 1:2], EPS, None, ALU.add).then_inc(s_gnve, 1)

            def gn_apply(r):
                dve.wait_ge(s_gnrs, r + 1)
                dve.tensor_scalar(xnT[:, r], xbank[r][:, 0:TW], gn_mv[:, r, 0:1], gn_rs[:, r:r + 1],
                                  ALU.subtract, ALU.mult).then_inc(s_xnT, 1)

            def weights_1():
                dve.wait_ge(s_const, 2)
                dve.wait_ge(s_wout, 32)
                for b in range(G):
                    dve.tensor_copy(ctxo[:, b, :, P:P + HEADS],
                                    blockmask[:, :, 0:1].rearrange("p h o -> p o h").broadcast_to([P, G, HEADS]))
                link(dve.tensor_reduce(wout_sum[:], wout_sb[:], AX_X, ALU.add))
                link(dve.tensor_scalar(wout_sum[:], wout_sum[:], 1.0 / C, None, ALU.mult))
                link(dve.tensor_scalar(wout_c[:], wout_sb[:], wout_sum[:, 0:1], ATTN_SCALE, ALU.subtract, ALU.mult))
                dve.tensor_tensor(wout_bd[:], wout_c[:, None, :].broadcast_to([P, HEADS, C]), blockmask[:],
                                  ALU.mult).then_inc(s_wprep, 1)
                link(dve.tensor_reduce(bsum[C:C + 1, :], brow[C:C + 1, :], AX_X, ALU.add))
                link(dve.tensor_scalar(bsum[C:C + 1, :], bsum[C:C + 1, :], 1.0 / C, None, ALU.mult))
                dve.tensor_scalar(proj[C:C + 1, 0:C], brow[C:C + 1, :], bsum[C:C + 1, 0:1], None, ALU.subtract)
                dve.memset(proj[C:C + 1, P:P + 1], 1.0)

            def weights_2():
                dve.wait_ge(s_wpe, 1)
                dve.tensor_copy(wv_t[:], bank[7][:, 0:C]).then_inc(s_wev, 1)

            def weights_3():
                dve.wait_ge(s_wpe, 2)
                dve.tensor_copy(proj[0:C, 0:P], bank[7][0:C, 0:P]).then_inc(s_wev, 1)

            def weights_4():
                dve.wait_ge(s_small4, 1)
                dve.tensor_tensor(small_bd[:], small4[:, 0:5 * C].rearrange("p (n c) -> p n c", n=5)[:, :, None, :]
                                  .broadcast_to([P, 5, G, C]), blockmask[:, None].broadcast_to([P, 5, G, C]),
                                  ALU.mult).then_inc(s_wprep, 1)

            def weights_5():
                dve.wait_ge(s_wpe, 3)
                dve.tensor_scalar(score_bd[:], bank[7][:, 0:P], ATTN_SCALE, None, ALU.mult)
                dve.tensor_copy(wvT_bd[:], bank[7][:, P:2 * P])
                dve.tensor_copy(wT_bd[:], bank[7][:, 2 * P:3 * P])
                dve.tensor_copy(vT_bd[:], bank[7][:, 3 * P:4 * P]).then_inc(s_wev, 1)
                dve.memset(v1[:, :, :, :, C + 1:], 0.0)
                dve.memset(v1[:, :, :, :, C:C + 1], 1.0)
                dve.memset(warm[:, :, :, 0:LEAD], 0.0).then_inc(s_rows, 1)

            def max_a(r):
                for g in range(G):
                    dve.wait_ge(s_maxA, r * G + g + 1)
                    dve.tensor_reduce(qmax_b[:, r, :, g, :],
                                      bank[g][:, 0:256].rearrange("p (h e d) -> p h e d", h=2, d=C), AX_X, ALU.max)
                    dve.tensor_reduce(kmax_b[:, r, g:g + 1], bank[g][:, 256:512], AX_X, ALU.max).then_inc(s_redA, 1)

            def shift_a(r):
                dve.wait_ge(s_negA, r + 1)
                dve.tensor_copy(qshift[0:32, r], neg_banks(r)[0][0:32, 384:])
                dve.tensor_copy(kshift[0:G, r], neg_banks(r)[1][0:G, 256:384]).then_inc(s_shA, 1)

            def contexts(r):
                m = [bank[5 + half][:, 0:272].rearrange("p (g n) -> p g n", g=2) for half in range(2)]
                for half in range(2):
                    dve.wait_ge(s_ctx, 2 * r + half + 1)
                    ins = dve.reciprocal(ksum_r[:, r, 2 * half:2 * half + 2], m[half][:, :, P])
                link(ins)
                for g in range(G):
                    ins = dve.scalar_tensor_tensor(
                        out=ctxo[:, r, g, 0:P], in0=m[g // 2][:, g % 2, 0:P], scalar=ksum_r[:, r, g:g + 1],
                        in1=blockmask[:].rearrange("p h c -> p (h c)"), op0=ALU.mult, op1=ALU.mult)
                    if g % 2:
                        ins.then_inc(s_ctxS, 1)

            def heads(r, gs):
                for g in gs:
                    dve.wait_ge(s_out, r * G + g + 1)
                    o = bank[(7, 4)[g % 2]][:, 0:264].rearrange("p (h n) -> p h n", h=2)
                    rq = qsum_r[:, r, g].rearrange("p (h e) -> p h e", h=2)
                    link(dve.reciprocal(rq, o[:, :, P:P + HEADS]))
                    dve.tensor_tensor(z4[:, r].rearrange("p (h g) (e c) -> p g h e c", h=2, e=HEADS)[:, g],
                                      o[:, :, 0:P].rearrange("p h (e c) -> p h e c", e=HEADS),
                                      rq[:, :, :, None].broadcast_to([P, 2, HEADS, C]), ALU.mult).then_inc(s_z4, 1)

            def bc(t):
                return t[:, :, None].broadcast_to([P, G * HALVES, C])

            def variance(n, r):
                dve.wait_ge(s_sq[n], r + 1)
                link(dve.tensor_reduce(ln_sum[:, n, r], sq[:, n % 2, r], AX_X, ALU.add))
                dve.tensor_scalar(ln_ve[:, n, r], ln_sum[:, n, r], 1.0 / C, EPS, ALU.mult, ALU.add).then_inc(s_ve[n], 1)

            def center(n, src, r):
                link(dve.tensor_reduce(ln_mean[:, n, r], src[:, r], AX_X, ALU.add))
                link(dve.tensor_scalar(ln_mean[:, n, r], ln_mean[:, n, r], 1.0 / C, None, ALU.mult))
                dve.tensor_tensor(tc[:, n - 1, r], src[:, r], bc(ln_mean[:, n, r]), ALU.subtract).then_inc(s_sqin[n], 1)

            def normalize(n, r):
                if n == 2 and r >= 2:
                    dve.wait_ge(s_sd, r - 1)
                    link(dve.reciprocal(ln_rs[:, n, r], ln_sd[:, r]))
                else:
                    dve.wait_ge(s_rs[n], r + 1)
                dve.tensor_tensor(tn[:, n - 1, r].rearrange("p h g c -> p (h g) c"), tc[:, n - 1, r],
                                  bc(ln_rs[:, n, r]), ALU.mult).then_inc(s_tn[n - 1], 1)

            def gain(r):
                dve.wait_ge(s_t1, r + 1)
                center(1, t1, r)

            def max_b(r):
                for g in range(G):
                    dve.wait_ge(s_maxB, r * G + g + 1)
                    dve.tensor_reduce(smax_b[:, r, 0, g:g + 1], bank[g][:, 0:P], AX_X, ALU.max)
                    dve.tensor_reduce(smax_b[:, r, 1, g:g + 1], bank[g][:, P:3 * P], AX_X, ALU.max).then_inc(s_redB, 1)

            def shift_b(r):
                dve.wait_ge(s_negB, r + 1)
                dve.tensor_copy(sshift[0:8, r], bank[5][0:8, 0:P]).then_inc(s_shB, 1)

            def attend(r):
                dve.wait_ge(s_pvk, r + 1)
                pv = vbank[r][:].rearrange("p (k n) -> p k n", n=2 * C)
                link(dve.reciprocal(psum_r[:, r], pv[:, :, C]))
                dve.tensor_tensor(attn[:, r], pv[:, :, 0:C], bc(psum_r[:, r]), ALU.mult).then_inc(s_attn, 1)

            def add_attention(r):
                dve.wait_ge(s_attn, r + 1)
                link(dve.tensor_tensor(t2[:, r], attn[:, r], t1[:, r], ALU.add))
                center(2, t2, r)

            def wx_stats(r):
                dve.wait_ge(s_wx if r == R - 1 else s_wxS, r + 1)
                dve.bn_stats(bn_stats[:, r], wbank[r][:, 0:TW] if r == R - 1 else wxT[:, r]).then_inc(s_bnst, 1)

            gn_stats_of(0)
            dve.wait_ge(s_wqk4, 1)
            dve.tensor_copy(wqk4_b[:], wqk4[:]).then_inc(s_wqkb, 1)
            gn_apply(0)
            dve.wait_ge(s_xnT, 1)
            dve.tensor_copy(xnT_b[:, 0], xnT[:, 0]).then_inc(s_xnTb, 1)
            gn_stats_of(1)
            gn_apply(1)
            gn_stats_of(2)
            max_a(0)
            weights_2()
            gn_apply(2)
            shift_a(0)
            gn_stats_of(3)
            weights_1()
            gn_apply(3)
            weights_3()
            for r in range(R):
                if r == 3:
                    normalize(1, 0)
                if r >= 1:
                    contexts(r - 1)
                if r == 2:
                    variance(0, 0)
                if r + 1 < R:
                    max_a(r + 1)
                if r == 0:
                    weights_4()
                if r >= 1:
                    heads(r - 1, (0,))
                if r + 1 < R:
                    shift_a(r + 1)
                if r == 0:
                    weights_5()
                if r == 2:
                    gain(0)
                if r >= 1:
                    heads(r - 1, (1,))
                if r == 2:
                    variance(1, 0)
                if r == 3:
                    variance(0, 1)
                if r >= 1:
                    heads(r - 1, (2,))
                if r >= 1:
                    heads(r - 1, (3,))
            max_b(0)
            gain(1)
            shift_b(0)
            variance(1, 1)
            variance(0, 2)
            contexts(3)
            normalize(1, 1)
            heads(3, range(G))
            gain(2)
            max_b(1)
            variance(1, 2)
            shift_b(1)
            normalize(1, 2)
            variance(0, 3)
            gain(3)
            variance(1, 3)
            max_b(2)
            normalize(1, 3)
            attend(0)
            shift_b(2)
            add_attention(0)
            variance(2, 0)
            normalize(2, 0)
            max_b(3)
            attend(1)
            shift_b(3)
            add_attention(1)
            wx_stats(0)
            variance(2, 1)
            normalize(2, 1)
            attend(2)
            add_attention(2)
            attend(3)
            variance(2, 2)
            add_attention(3)
            normalize(2, 2)
            variance(2, 3)
            wx_stats(1)
            normalize(2, 3)
            wx_stats(2)
            wx_stats(3)

            dve.wait_ge(s_bnst, R)
            link(dve.bn_aggr(bn_mv[:], bn_stats[:].rearrange("p r n -> p (r n)")))
            dve.scalar_tensor_tensor(out=bn_mv[:, 1:2], in0=bn_mv[:, 0:1], scalar=bn_mv[:, 0:1], in1=bn_mv[:, 1:2],
                                     op0=ALU.mult, op1=ALU.add).then_inc(s_bnin, 1)
            dve.wait_ge(s_bnp, 1)
            dve.tensor_scalar(bn_sc[:, 2:3], bank[6][:, 0:1], -1.0, None, ALU.mult)
            link(dve.tensor_scalar(bn_sc[:, 3:4], bank[6][:, 1:2], EPS, None, ALU.add))
            dve.scalar_tensor_tensor(out=bn_sc[:, 0:1], in0=bank[6][:, 0:1], scalar=bn_sc[:, 2:3],
                                     in1=bn_sc[:, 3:4], op0=ALU.mult, op1=ALU.add).then_inc(s_bnve, 1)
            dve.wait_ge(s_bnrs, 1)
            link(dve.tensor_tensor(bn_sc[:, 4:5], bn_sc[:, 1:2], gam4, ALU.mult))
            dve.scalar_tensor_tensor(out=bn_sc[:, 6:7], in0=bn_sc[:, 4:5], scalar=bn_sc[:, 2:3], in1=bet4,
                                     op0=ALU.mult, op1=ALU.add).then_inc(s_bnsc, 1)
            dve.wait_ge(s_bnsc, 1)
            dve.wait_ge(s_wxS, R)
            for s in range(1, STRIDE + 1):
                m = place(s)[0]
                dve.tensor_scalar(wxn[:, m], wxT[:].rearrange("p r (j m) -> p m r j", m=STRIDE)[:, m],
                                  bn_sc[:, 4:5], bn_sc[:, 6:7], ALU.mult, ALU.add).then_inc(s_wxn, 1)

            def residual(time):
                for r in range(R):
                    dve.wait_ge(s_yT, time * R + r + 1)
                    dve.tensor_tensor(
                        out_tok[:, r].rearrange("p g h c -> p h g c"),
                        bank[4 + r][:, 0:TW].rearrange("p (h g c) -> p h g c", h=HALVES, g=G),
                        t2[:, r].rearrange("p (h g) c -> p h g c", h=HALVES), ALU.add).then_inc(s_fin, 1)

            dve.memset(state[:, :, STRIDE - 1:], 0.0).then_inc(s_state, 1)
            residual(0)
            link(dve.tensor_tensor(diff[:], warm[:, WARM - 1, :, 1:], ys[:, :, 0:CHUNKS - 1, STRIDE - 1], ALU.subtract))
            link(dve.tensor_tensor(diff[:], diff[:], diff[:], ALU.mult))
            link(dve.tensor_reduce(worst[:, 0:1], diff[:].rearrange("p r j -> p (r j)"), AX_X, ALU.max))
            dve.tensor_scalar(worst[:, 1:2], worst[:, 0:1], AGREE ** 2, None, ALU.is_gt).then_inc(s_worst, 1)
            dve.wait_ge(s_votes, 1)
            dve.tensor_copy(again[:], bank[0][0:1, 0:1]).then_inc(s_flag, 1)
            with step_by_step(dve):
                dve.wait_ge(s_stored, 16 * R)
                residual(1)

        @block.tensor
        def _(pe):
            def rows(t, g):
                return t[C * g:C * (g + 1)]

            def keep_awake(place_of_wait, at=7):
                for _ in range(KEEP[place_of_wait]):
                    pe.matmul(bank[at][:], idle_b[:, 0:P], idle_b[:], start=True, stop=True)

            rep = rep_id[:].rearrange("p g c -> p (g c)")

            def x_in(r):
                pe.wait_ge(s_x[r], 16 * HALVES)
                if r == 3:
                    pe.wait_ge(s_xn1, 2)
                for h in range(HALVES):
                    ins = pe.transpose(xbank[r][:, h * P:(h + 1) * P], x_tok[:, h, r].rearrange("p g c -> p (g c)"),
                                       ident[:])
                ins.then_inc(s_xT, 1)

            def x_back(r):
                pe.wait_ge(s_xnT, r + 1)
                for h in range(HALVES):
                    ins = pe.transpose(xbank[r][:, h * P:(h + 1) * P], xnT[:, r, h * P:(h + 1) * P], ident[:])
                ins.then_inc(s_xnk, 1)

            def value_weights():
                pe.transpose(bank[7][:, 0:C], w_raw[:, 2 * P:3 * P], ident[0:C, 0:C]).then_inc(s_wpe, 1)

            def projection():
                pe.wait_ge(s_wev, 1)
                pe.wait_ge(s_wprep, 1)
                pe.matmul(bank[7][0:C, 0:P], wv_t[:], wout_bd[:].rearrange("p h c -> p (h c)"),
                          start=True, stop=True).then_inc(s_wpe, 1)

            def small_rows():
                pe.wait_ge(s_wsmall, 16 * 7)
                pe.wait_ge(s_wev, 2)
                pe.matmul(bank[7][:, 0:5 * C + 2], rep, w_raw[:, 3 * P:], start=True, stop=True).then_inc(s_rep, 1)

            def small_blocks():
                pe.wait_ge(s_wprep, 2)
                bd = [small_bd[:, n].rearrange("p g c -> p (g c)") for n in range(5)]
                pe.matmul(bank[7][:, 0:P], bd[0], bd[1], start=True, stop=True)
                for n in range(3):
                    ins = pe.transpose(bank[7][:, (n + 1) * P:(n + 2) * P], bd[2 + n], ident[:])
                ins.then_inc(s_wpe, 1)

            def max_a(r):
                if r == 0:
                    pe.wait_ge(s_wqkb, 1)
                pe.wait_ge(s_xnTb, r + 1)
                for h in range(HALVES):
                    for g in range(G):
                        if r and h == 0:
                            pe.wait_ge(s_expA, (r - 1) * G + g + 1)
                        pe.matmul(bank[g][:, h * P:(h + 1) * P], rows(xnT_b, g)[:, r, h * P:(h + 1) * P],
                                  rows(wqk4_b, g)[:, 0:P], start=True, stop=True)
                for g in range(G):
                    pe.matmul(bank[g][:, 256:512], rows(wqk4_b, g)[:, P:2 * P], rows(xnT_b, g)[:, r, :],
                              start=True, stop=True).then_inc(s_maxA, 1)

            def neg_a(r):
                if r == 0:
                    pe.wait_ge(s_wev, 1)
                if r == 1:
                    pe.wait_ge(s_xn1, R)
                pe.wait_ge(s_redA, G * (r + 1))
                pe.matmul(neg_banks(r)[0][0:32, 384:], qmax_b[:, r].rearrange("p h g e -> p (h g e)"), negid_b[:],
                          start=True, stop=True)
                pe.matmul(neg_banks(r)[1][0:G, 256:384], kmax_b[:, r], negid_b[:], start=True, stop=True).then_inc(s_negA, 1)

            def queries(r):
                for g in range(G):
                    if r == 0 and g % 2 == 0:
                        pe.wait_ge(s_xn1, 1)
                        keep_awake("queries 0", at=4)
                    if r == 1 and g % 2 == 0:
                        pe.wait_ge(s_xn1, 3)
                        keep_awake("queries 1", at=6)
                    pe.wait_ge(s_redA, r * G + g + 1)
                    pe.matmul(bank[g][:, 0:256], rows(wqk4, g)[:, 0:P], rows(xnT, g)[:, r, :],
                              start=True, stop=True)

            def keys(r, h):
                if r + h <= 1:
                    keep_awake(f"keys {r}", at=(4, 6)[r])
                for g in range(G):
                    pe.matmul(bank[g][:, 256 + h * P:256 + (h + 1) * P], rows(xnT, g)[:, r, h * P:(h + 1) * P],
                              rows(wqk4, g)[:, P:2 * P], start=False, stop=True, skip_group_check=True)

            def shifts_a(r):
                pe.wait_ge(s_shA, r + 1)
                if r == 0:
                    pe.wait_ge(s_const, 1)
                for g in range(G):
                    for h in range(HALVES):
                        pe.matmul(bank[g][:, h * P:(h + 1) * P], sel32[:, h * G + g, :], qshift[:, r],
                                  start=False, stop=True, skip_group_check=True)
                    for h in range(HALVES):
                        ins = pe.matmul(bank[g][:, 256 + h * P:256 + (h + 1) * P], sel4[:, g, :], kshift[:, r],
                                        start=False, stop=True, skip_group_check=True)
                    ins.then_inc(s_qk, 1)

            def grams(r):
                if r == 0:
                    pe.wait_ge(s_xn1, 1)
                if r == R - 1:
                    pe.wait_ge(s_z4, G * r)
                elif r >= 2:
                    pe.wait_ge(s_z4, G * (r - 1))
                for g in range(G):
                    pe.wait_ge(s_expA, r * G + g + 1)
                    for h in range(HALVES):
                        ins = pe.matmul(bank[4][0:C + 1, g * P:(g + 1) * P], xn1[:, r, h, g, :],
                                        eqk[:, r, g, 256 + h * P:256 + (h + 1) * P], start=(h == 0), stop=(h == 1))
                ins.then_inc(s_gram, 1)

            def contexts(r):
                pe.wait_ge(s_gramS, r + 1)
                if r == 0:
                    pe.wait_ge(s_wev, 2)
                for g in range(G):
                    ins = pe.matmul(bank[5 + g // 2][:, 136 * (g % 2):136 * (g % 2) + P + 1],
                                    gram[:, r, g * P:(g + 1) * P], proj[:], start=True, stop=True)
                    if g % 2:
                        ins.then_inc(s_ctx, 1)

            def outs(r, gs):
                if r == 0 and gs and gs[0] == 0:
                    pe.wait_ge(s_wev, 3)
                for g in gs:
                    pe.wait_ge(s_ctxS, 2 * r + g // 2 + 1)
                    if r * G + g >= 2:
                        pe.wait_ge(s_z4, r * G + g - 1)
                    if g == 1 and r + 2 < R:
                        pe.wait_ge(s_gramS, r + 2)
                    for h in range(HALVES):
                        ins = pe.matmul(bank[(7, 4)[g % 2]][:, h * 132:(h + 1) * 132], eqk[:, r, g, h * P:(h + 1) * P],
                                        ctxo[:, r, g, :], start=True, stop=True)
                    ins.then_inc(s_out, 1)

            def turn(r):
                if r == 0:
                    pe.wait_ge(s_z4, 2 * G)
                elif r == 1:
                    pe.wait_ge(s_ctxS, 2 * R)
                if r:
                    pe.wait_ge(s_tnTb, r)
                    pe.wait_ge(s_shB, r)
                pe.wait_ge(s_tn[0], r + 1)
                for h in range(HALVES):
                    ins = pe.transpose(tbank[r][:, h * P:(h + 1) * P], tn[:, 0, r, h].rearrange("p g c -> p (g c)"),
                                       ident[:])
                ins.then_inc(s_T, 1)

            def project(r):
                if r:
                    pe.wait_ge(s_v1, r)
                else:
                    pe.wait_ge(s_ctxS, 6)
                pe.wait_ge(s_tnT, r + 1)
                pe.matmul(bank[6][:, 0:TW], score_bd[:], tnT[:, r], start=True, stop=True)
                for h in range(HALVES):
                    ins = pe.matmul(bank[6][:, 256 + h * P:256 + (h + 1) * P], tnT[:, r, h * P:(h + 1) * P],
                                    wvT_bd[:], start=True, stop=True)
                ins.then_inc(s_u, 1)

            def max_b(r):
                if r == 0:
                    pe.wait_ge(s_const, 3)
                pe.wait_ge(s_tnTb, r + 1)
                pe.wait_ge(s_uTb, r + 1)
                if r:
                    pe.wait_ge(s_expB, r * G)
                else:
                    pe.wait_ge(s_expA, R * G)
                for h in range(HALVES):
                    for g in range(G):
                        pe.matmul(bank[g][:, h * P:h * P + (h + 1) * P], rows(uT_b, g)[:, r, h * P:(h + 1) * P],
                                  rows(tnT_b, g)[:, r, 0:(h + 1) * P], start=(h == 0), stop=True,
                                  skip_group_check=(h == 1))
                for g in range(G):
                    for h in range(HALVES):
                        ins = pe.matmul(bank[g][:, 2 * h * P:(2 * h + 1) * P], ident_b[:], mask_ts[:],
                                        start=False, stop=True, skip_group_check=True)
                    ins.then_inc(s_maxB, 1)

            def neg_b(r):
                pe.wait_ge(s_redB, G * (r + 1))
                if r:
                    pe.wait_ge(s_tnTb, r + 1)
                pe.matmul(bank[5][0:8, 0:P], smax_b[:, r].rearrange("p h g -> p (h g)"), negid_b[:],
                          start=True, stop=True).then_inc(s_negB, 1)

            def scores(r, ks):
                if ks == 0:
                    pe.wait_ge(s_uT, r + 1)
                for g in range(G):
                    pe.wait_ge(s_redB, r * G + g + 1)
                    pe.matmul(bank[g][:, 256 * ks:256 * ks + TW - ks * P], rows(tnT, g)[:, r, ks * P:(ks + 1) * P],
                              rows(uT, g)[:, r, ks * P:TW], start=(ks == 0), stop=True,
                              skip_group_check=(ks == 1))

            def masks(r):
                for g in range(G):
                    for ks in range(HALVES):
                        pe.matmul(bank[g][:, 256 * ks:256 * ks + P], ident_b[:], mask_st[:],
                                  start=False, stop=True, skip_group_check=True)

            def shifts_b(r):
                pe.wait_ge(s_shB, r + 1)
                for g in range(G):
                    for ks in range(HALVES):
                        for qs in range(ks, HALVES):
                            at = 256 * ks + (qs - ks) * P
                            ins = pe.matmul(bank[g][:, at:at + P], sel8[:, qs * G + g, :], sshift[:, r],
                                            start=False, stop=True, skip_group_check=True)
                    ins.then_inc(s_st, 1)

            def values(r, b):
                if r == 0:
                    pe.wait_ge(s_z4, G * R)
                elif r < 3:
                    pe.wait_ge(s_attn, r)
                else:
                    pe.wait_ge(s_shB, R)
                pe.wait_ge(s_v1, r + 1)
                for g in (2 * b, 2 * b + 1):
                    pe.wait_ge(s_expB, r * G + g + 1)
                    for ks in range(HALVES):
                        ins = pe.matmul(vbank[r][64 * (g % 2):64 * (g % 2) + 64, b * TW + ks * P:(b + 1) * TW],
                                        v1[:, r, ks, g, :], probsT[:, r, g, 256 * ks:TW + ks * P],
                                        start=(ks == 0), stop=(ks == 1))
                ins.then_inc(s_pv, 1)

            def values_back(r):
                pe.wait_ge(s_pvT, r + 1)
                for h in range(HALVES):
                    for b in range(2):
                        ins = pe.transpose(vbank[r][:, (2 * h + b) * P:(2 * h + b + 1) * P],
                                           pvT[:, r, b, h * P:(h + 1) * P], ident[:])
                ins.then_inc(s_pvk, 1)

            def turn_2(r):
                pe.wait_ge(s_tn[1], r + 1)
                if r == 3:
                    pe.wait_ge(s_attn, 3)
                elif r:
                    pe.wait_ge(s_wxS, r)
                for h in range(HALVES):
                    ins = pe.transpose(wbank[r][:, h * P:(h + 1) * P], tn[:, 1, r, h].rearrange("p g c -> p (g c)"),
                                       ident[:])
                ins.then_inc(s_T2, 1)

            def ffn(r):
                pe.wait_ge(s_tn2T, r + 1)
                pe.matmul(wbank[r][:, 0:TW], wT_bd[:], tn2T[:, r], start=True, stop=True).then_inc(s_wx, 1)

            pe.wait_ge(s_idle, 1)
            keep_awake("inputs")
            pe.wait_ge(s_ident, 2)
            x_in(0)
            pe.wait_ge(s_wraw, 16)
            pe.matmul(bank[0][:, 0:2 * P], rep, w_raw[:, 0:2 * P], start=True, stop=True).then_inc(s_rep, 1)
            x_in(1)
            keep_awake("input 1")
            x_in(2)
            keep_awake("input 2")
            x_back(0)
            pe.wait_ge(s_wqk4, 1)
            max_a(0)
            x_back(1)
            keep_awake("value weights")
            value_weights()
            queries(0)
            neg_a(0)
            x_back(2)
            keys(0, 0)
            x_in(3)
            keys(0, 1)
            shifts_a(0)
            projection()
            for r in range(R):
                if r >= 1:
                    contexts(r - 1)
                if r + 1 < R:
                    max_a(r + 1)
                    if r == 0:
                        x_back(3)
                        small_rows()
                    grams(r)
                    outs(r - 1, (0,) if r else ())
                    queries(r + 1)
                    neg_a(r + 1)
                    outs(r - 1, (1,) if r else ())
                    keys(r + 1, 0)
                    outs(r - 1, (2,) if r else ())
                    if r == 0:
                        small_blocks()
                    keys(r + 1, 1)
                    outs(r - 1, (3,) if r else ())
                    shifts_a(r + 1)
                else:
                    turn(0)
                    outs(r - 1, (0,))
                    pe.wait_ge(s_tnTb, 1)
                    outs(r - 1, (1,))
                    project(0)
                    outs(r - 1, (2, 3))
                    max_b(0)
                    grams(r)
            scores(0, 0)
            neg_b(0)
            scores(0, 1)
            pe.wait_ge(s_v1, 1)
            pe.wait_ge(s_shB, 1)
            contexts(3)
            masks(0)
            shifts_b(0)
            outs(3, (0, 1))
            for r in range(R):
                if r == 0:
                    turn(1)
                    outs(3, (2, 3))
                else:
                    values(r - 1, 0)
                if r == 0:
                    pe.wait_ge(s_v1, 1)
                    keep_awake("projection 1", at=6)
                if r == 1:
                    keep_awake("projection 2", at=4)
                if r + 1 < R:
                    project(r + 1)
                if r == 0:
                    pe.wait_ge(s_expB, G)
                    keep_awake("weights 0", at=3)
                if r >= 1:
                    values(r - 1, 1)
                if r + 1 < R:
                    max_b(r + 1)
                if r == 2:
                    turn_2(0)
                if r == 3:
                    values(3, 0)
                if r >= 1:
                    values_back(r - 1)
                if r == 2:
                    ffn(0)
                if r + 1 < R:
                    scores(r + 1, 0)
                    neg_b(r + 1)
                    scores(r + 1, 1)
                    if r == 0:
                        pe.wait_ge(s_z4, G * R)
                        keep_awake("turn 2", at=7)
                    if r + 2 < R:
                        turn(r + 2)
                    masks(r + 1)
                    shifts_b(r + 1)
            values(3, 1)
            turn_2(1)
            values_back(3)
            ffn(1)
            keep_awake("second turns", at=3)
            for r in range(2, R):
                turn_2(r)
                keep_awake("second turn", at=3)
                ffn(r)

            keep_awake("batch statistics", at=3)
            pe.wait_ge(s_bnin, 1)
            pe.matmul(bank[6][:, 0:2], groupavg[:].rearrange("p g c -> p (g c)"), bn_mv[:],
                      start=True, stop=True).then_inc(s_bnp, 1)

            keep_awake("scan", at=3)
            def part(c, s):
                return bank[2 * c + s % 2][:, 0:RPC * CHUNKS].rearrange("p (r j) -> p r j", r=RPC)

            def inputs(c, s):
                m, at, j0 = place(s)
                if s >= 3:
                    pe.wait_ge(s_y[c], s - 1)
                if s <= STRIDE:
                    pe.wait_ge(s_wxn, s)
                pe.matmul(part(c, s)[:, :, j0:], ident[:], wxn[:, m, c * RPC:(c + 1) * RPC, j0 + at:CHUNKS + at],
                          start=True, stop=False)

            for c in range(CHAINS):
                inputs(c, 1)
            for s in range(1, STEPS):
                j0 = place(s)[2]
                for c in range(CHAINS):
                    rr = slice(c * RPC, (c + 1) * RPC)
                    src = warm[:, s - 1, rr, j0:] if s <= WARM else ys[:, rr, :, s - 1 - WARM]
                    pe.wait_ge(s_y[c], s)
                    pe.matmul(part(c, s)[:, :, j0:], vT_bd[:], src, start=False, stop=True).then_inc(s_pre[c], 1)
                    if s + 1 < STEPS:
                        inputs(c, s + 1)

            def back(time):
                for r in range(R):
                    if time:
                        pe.wait_ge(s_fin, R)
                    else:
                        pe.wait_ge(s_y[r // RPC], STEPS)
                    for h in range(HALVES):
                        js = slice(h * CHUNKS // 2, (h + 1) * CHUNKS // 2)
                        ins = pe.transpose(bank[4 + r][:, h * P:(h + 1) * P],
                                           ys[:, r, js].rearrange("p j m -> p (j m)"), ident[:])
                    ins.then_inc(s_yT, 1)

            back(0)
            pe.wait_ge(s_worst, 1)
            pe.matmul(bank[0][0:1, 0:1], worst[:, 1:2], ones_f[:], start=True, stop=True).then_inc(s_votes, 1)
            with step_by_step(pe):
                with pe.Fori(0, CHUNKS) as j:
                    for m in range(STRIDE):
                        pe.matmul(bank[m % 4][:, 0:R], ident[:], wxn[:, m, :, bass.ds(j, 1)], start=True, stop=False)
                        pe.wait_ge(s_state, j * STRIDE + (m + 1))
                        pe.matmul(bank[m % 4][:, 0:R], vT_bd[:], state[:, :, (m + STRIDE - 1) % STRIDE],
                                  start=False, stop=True).then_inc(s_mm, 1)
                pe.wait_ge(s_kept, CHUNKS + 1)
                back(1)


_INS = ["x", "L0_conv_w_qkv", "L0_conv_w_out", "L0_conv_b_out", "L0_conv_g_ln", "L0_conv_b_ln", "L1_attn_Wq",
        "L1_attn_Wk", "L1_attn_Wv", "L1_ffn_W", "L1_ffn_V", "L1_ffn_gamma", "L1_ffn_beta"]


def kernel(**inputs):
    import concourse.bacc as _bacc
    from concourse.bass_utils import run_bass_kernel_spmd as _run

    nc = _bacc.Bacc("TRN2", target_bir_lowering=False, num_devices=1)
    arrays, args = {}, []
    for name in _INS:
        a = np.ascontiguousarray(inputs[name])
        arrays[f"in_{name}_dram"] = a
        args.append(nc.dram_tensor(f"in_{name}_dram", a.shape, mybir.dt.from_np(a.dtype), kind="ExternalInput").ap())
    shape = np.asarray(inputs["x"]).shape
    args.append(nc.dram_tensor("out_0_dram", shape, F32, kind="ExternalOutput").ap())
    conv_attn_rnn(nc, *args)
    r = _run(nc, [arrays], core_ids=[0])
    return r.results[0]["out_0_dram"]
```
